# Optimizing a Trainium2 kernel written in Bass

```python
import numpy as np
import jax
import jax.numpy as jnp

def _softmax(x, axis=-1):
    return jax.nn.softmax(x, axis=axis)

def _gelu(x):
    return jax.nn.gelu(x, approximate=True)

def _silu(x):
    return jax.nn.silu(x)

def _sigmoid(x):
    return jax.nn.sigmoid(x)

def _layernorm(x, axis=-1, eps=1e-05):
    m = jnp.mean(x, axis=axis, keepdims=True)
    v = jnp.var(x, axis=axis, keepdims=True)
    return (x - m) / jnp.sqrt(v + eps)

def _scatter_add(tgt, idx, src, axis=0):
    return tgt.at[idx].add(src)

def _segment_sum(src, seg, n):
    return jax.ops.segment_sum(src, seg, n)
kernel_name = 'mk_dlrm_tower_d1_rec_r8_13831d'

def setup_inputs(seed: int=0):
    np.random.seed(seed)
    _w = jnp.asarray

    def _rec_inputs():
        import jax
        import jax.numpy as jnp
        _tk = jax.random.key(seed)
        dense_ctx = jax.random.normal(jax.random.fold_in(_tk, 190), (512, 16), jnp.float32)
        ids = jnp.stack([jax.random.randint(jax.random.fold_in(_tk, 200 + f), (512,), 0, v, jnp.int32) for f, v in enumerate([125000, 12500, 12500, 1000, 1250, 1000, 1000, 1250, 125000, 1250, 1000, 1250, 12500, 1000, 1250, 12500, 1250, 1250, 125000, 1250, 125000, 1250, 125000, 12500, 12500, 125000, 1000, 1250, 125000, 1250, 12500, 125000, 1250, 125000, 1250, 125000, 125000, 125000, 1250])], axis=1)
        tbl_0 = 0.05 * jax.random.normal(jax.random.fold_in(_tk, 500 + 0), (125000, 16), jnp.float32)
        tbl_1 = 0.05 * jax.random.normal(jax.random.fold_in(_tk, 500 + 1), (12500, 16), jnp.float32)
        tbl_2 = 0.05 * jax.random.normal(jax.random.fold_in(_tk, 500 + 2), (12500, 16), jnp.float32)
        tbl_3 = 0.05 * jax.random.normal(jax.random.fold_in(_tk, 500 + 3), (1000, 16), jnp.float32)
        tbl_4 = 0.05 * jax.random.normal(jax.random.fold_in(_tk, 500 + 4), (1250, 16), jnp.float32)
        tbl_5 = 0.05 * jax.random.normal(jax.random.fold_in(_tk, 500 + 5), (1000, 16), jnp.float32)
        tbl_6 = 0.05 * jax.random.normal(jax.random.fold_in(_tk, 500 + 6), (1000, 16), jnp.float32)
        tbl_7 = 0.05 * jax.random.normal(jax.random.fold_in(_tk, 500 + 7), (1250, 16), jnp.float32)
        tbl_8 = 0.05 * jax.random.normal(jax.random.fold_in(_tk, 500 + 8), (125000, 16), jnp.float32)
        tbl_9 = 0.05 * jax.random.normal(jax.random.fold_in(_tk, 500 + 9), (1250, 16), jnp.float32)
        tbl_10 = 0.05 * jax.random.normal(jax.random.fold_in(_tk, 500 + 10), (1000, 16), jnp.float32)
        tbl_11 = 0.05 * jax.random.normal(jax.random.fold_in(_tk, 500 + 11), (1250, 16), jnp.float32)
        tbl_12 = 0.05 * jax.random.normal(jax.random.fold_in(_tk, 500 + 12), (12500, 16), jnp.float32)
        tbl_13 = 0.05 * jax.random.normal(jax.random.fold_in(_tk, 500 + 13), (1000, 16), jnp.float32)
        tbl_14 = 0.05 * jax.random.normal(jax.random.fold_in(_tk, 500 + 14), (1250, 16), jnp.float32)
        tbl_15 = 0.05 * jax.random.normal(jax.random.fold_in(_tk, 500 + 15), (12500, 16), jnp.float32)
        tbl_16 = 0.05 * jax.random.normal(jax.random.fold_in(_tk, 500 + 16), (1250, 16), jnp.float32)
        tbl_17 = 0.05 * jax.random.normal(jax.random.fold_in(_tk, 500 + 17), (1250, 16), jnp.float32)
        tbl_18 = 0.05 * jax.random.normal(jax.random.fold_in(_tk, 500 + 18), (125000, 16), jnp.float32)
        tbl_19 = 0.05 * jax.random.normal(jax.random.fold_in(_tk, 500 + 19), (1250, 16), jnp.float32)
        tbl_20 = 0.05 * jax.random.normal(jax.random.fold_in(_tk, 500 + 20), (125000, 16), jnp.float32)
        tbl_21 = 0.05 * jax.random.normal(jax.random.fold_in(_tk, 500 + 21), (1250, 16), jnp.float32)
        tbl_22 = 0.05 * jax.random.normal(jax.random.fold_in(_tk, 500 + 22), (125000, 16), jnp.float32)
        tbl_23 = 0.05 * jax.random.normal(jax.random.fold_in(_tk, 500 + 23), (12500, 16), jnp.float32)
        tbl_24 = 0.05 * jax.random.normal(jax.random.fold_in(_tk, 500 + 24), (12500, 16), jnp.float32)
        tbl_25 = 0.05 * jax.random.normal(jax.random.fold_in(_tk, 500 + 25), (125000, 16), jnp.float32)
        tbl_26 = 0.05 * jax.random.normal(jax.random.fold_in(_tk, 500 + 26), (1000, 16), jnp.float32)
        tbl_27 = 0.05 * jax.random.normal(jax.random.fold_in(_tk, 500 + 27), (1250, 16), jnp.float32)
        tbl_28 = 0.05 * jax.random.normal(jax.random.fold_in(_tk, 500 + 28), (125000, 16), jnp.float32)
        tbl_29 = 0.05 * jax.random.normal(jax.random.fold_in(_tk, 500 + 29), (1250, 16), jnp.float32)
        tbl_30 = 0.05 * jax.random.normal(jax.random.fold_in(_tk, 500 + 30), (12500, 16), jnp.float32)
        tbl_31 = 0.05 * jax.random.normal(jax.random.fold_in(_tk, 500 + 31), (125000, 16), jnp.float32)
        tbl_32 = 0.05 * jax.random.normal(jax.random.fold_in(_tk, 500 + 32), (1250, 16), jnp.float32)
        tbl_33 = 0.05 * jax.random.normal(jax.random.fold_in(_tk, 500 + 33), (125000, 16), jnp.float32)
        tbl_34 = 0.05 * jax.random.normal(jax.random.fold_in(_tk, 500 + 34), (1250, 16), jnp.float32)
        tbl_35 = 0.05 * jax.random.normal(jax.random.fold_in(_tk, 500 + 35), (125000, 16), jnp.float32)
        tbl_36 = 0.05 * jax.random.normal(jax.random.fold_in(_tk, 500 + 36), (125000, 16), jnp.float32)
        tbl_37 = 0.05 * jax.random.normal(jax.random.fold_in(_tk, 500 + 37), (125000, 16), jnp.float32)
        tbl_38 = 0.05 * jax.random.normal(jax.random.fold_in(_tk, 500 + 38), (1250, 16), jnp.float32)
        _rk = jax.random.fold_in(_tk, 7)
        W_top1 = 0.05 * jax.random.normal(jax.random.fold_in(_tk, 801), (400, 512), jnp.float32)
        W_top2 = 0.0441942 * jax.random.normal(jax.random.fold_in(_tk, 802), (512, 256), jnp.float32)
        W_top3 = 0.0625 * jax.random.normal(jax.random.fold_in(_tk, 803), (256, 1), jnp.float32)
        b_top1 = jnp.zeros((512,), jnp.float32)
        b_top2 = jnp.zeros((256,), jnp.float32)
        return (dense_ctx, ids, tbl_0, tbl_1, tbl_2, tbl_3, tbl_4, tbl_5, tbl_6, tbl_7, tbl_8, tbl_9, tbl_10, tbl_11, tbl_12, tbl_13, tbl_14, tbl_15, tbl_16, tbl_17, tbl_18, tbl_19, tbl_20, tbl_21, tbl_22, tbl_23, tbl_24, tbl_25, tbl_26, tbl_27, tbl_28, tbl_29, tbl_30, tbl_31, tbl_32, tbl_33, tbl_34, tbl_35, tbl_36, tbl_37, tbl_38, W_top1, b_top1, W_top2, b_top2, W_top3)
    dense_ctx, ids, tbl_0, tbl_1, tbl_2, tbl_3, tbl_4, tbl_5, tbl_6, tbl_7, tbl_8, tbl_9, tbl_10, tbl_11, tbl_12, tbl_13, tbl_14, tbl_15, tbl_16, tbl_17, tbl_18, tbl_19, tbl_20, tbl_21, tbl_22, tbl_23, tbl_24, tbl_25, tbl_26, tbl_27, tbl_28, tbl_29, tbl_30, tbl_31, tbl_32, tbl_33, tbl_34, tbl_35, tbl_36, tbl_37, tbl_38, W_top1, b_top1, W_top2, b_top2, W_top3 = _rec_inputs()

    def _L0_rec_setup():
        import jax, jax.numpy as jnp
        import numpy as np
        B, F0, D = (256, 39, 16)
        CROSS = [128, 128, 128]
        key = jax.random.key(seed)
        k0, k1, k2, k3 = jax.random.split(key, 4)
        inputs = jax.random.normal(k0, (B, F0, D), dtype=jnp.float32)
        f0 = jax.random.normal(k1, (F0 * F0, CROSS[0]), dtype=jnp.float32) * 0.05
        f1 = jax.random.normal(k2, (CROSS[0] * F0, CROSS[1]), dtype=jnp.float32) * 0.05
        f2 = jax.random.normal(k3, (CROSS[1] * F0, CROSS[2]), dtype=jnp.float32) * 0.05
        return {'inputs': inputs, 'f0': f0, 'f1': f1, 'f2': f2}
    _L0_rec_all = _L0_rec_setup()
    _L0_rec_in = {k: v for k, v in _L0_rec_all.items() if k in ('f0', 'f1', 'f2')}
    del _L0_rec_all
    return {'dense_ctx': dense_ctx, 'ids': ids, 'tbl_0': tbl_0, 'tbl_1': tbl_1, 'tbl_2': tbl_2, 'tbl_3': tbl_3, 'tbl_4': tbl_4, 'tbl_5': tbl_5, 'tbl_6': tbl_6, 'tbl_7': tbl_7, 'tbl_8': tbl_8, 'tbl_9': tbl_9, 'tbl_10': tbl_10, 'tbl_11': tbl_11, 'tbl_12': tbl_12, 'tbl_13': tbl_13, 'tbl_14': tbl_14, 'tbl_15': tbl_15, 'tbl_16': tbl_16, 'tbl_17': tbl_17, 'tbl_18': tbl_18, 'tbl_19': tbl_19, 'tbl_20': tbl_20, 'tbl_21': tbl_21, 'tbl_22': tbl_22, 'tbl_23': tbl_23, 'tbl_24': tbl_24, 'tbl_25': tbl_25, 'tbl_26': tbl_26, 'tbl_27': tbl_27, 'tbl_28': tbl_28, 'tbl_29': tbl_29, 'tbl_30': tbl_30, 'tbl_31': tbl_31, 'tbl_32': tbl_32, 'tbl_33': tbl_33, 'tbl_34': tbl_34, 'tbl_35': tbl_35, 'tbl_36': tbl_36, 'tbl_37': tbl_37, 'tbl_38': tbl_38, 'W_top1': W_top1, 'b_top1': b_top1, 'W_top2': W_top2, 'b_top2': b_top2, 'W_top3': W_top3, 'L0_rec_f0': _L0_rec_in['f0'], 'L0_rec_f1': _L0_rec_in['f1'], 'L0_rec_f2': _L0_rec_in['f2']}

def reference(dense_ctx, ids, tbl_0, tbl_1, tbl_2, tbl_3, tbl_4, tbl_5, tbl_6, tbl_7, tbl_8, tbl_9, tbl_10, tbl_11, tbl_12, tbl_13, tbl_14, tbl_15, tbl_16, tbl_17, tbl_18, tbl_19, tbl_20, tbl_21, tbl_22, tbl_23, tbl_24, tbl_25, tbl_26, tbl_27, tbl_28, tbl_29, tbl_30, tbl_31, tbl_32, tbl_33, tbl_34, tbl_35, tbl_36, tbl_37, tbl_38, W_top1, b_top1, W_top2, b_top2, W_top3, L0_rec_f0, L0_rec_f1, L0_rec_f2):
    import jax
    import jax.numpy as jnp

    def _L0_rec_ref(inputs, f0, f1, f2):
        import jax, jax.numpy as jnp
        import numpy as np
        B, F0, D = (256, 39, 16)
        CROSS = [128, 128, 128]
        filters = [f0, f1, f2]
        x0 = inputs
        xk = inputs
        outs = []
        for W in filters:
            b, f, d = x0.shape
            g = xk.shape[1]
            z = jnp.einsum('bfd,bgd->bfgd', x0, xk).reshape(b, f * g, d)
            cur = jnp.einsum('bpd,pm->bmd', z, W)
            outs.append(cur)
            xk = cur
        result = jnp.concatenate(outs, axis=1)
        return jnp.sum(result, axis=-1)
    e = jnp.stack([tbl_0[ids[:, 0]], tbl_1[ids[:, 1]], tbl_2[ids[:, 2]], tbl_3[ids[:, 3]], tbl_4[ids[:, 4]], tbl_5[ids[:, 5]], tbl_6[ids[:, 6]], tbl_7[ids[:, 7]], tbl_8[ids[:, 8]], tbl_9[ids[:, 9]], tbl_10[ids[:, 10]], tbl_11[ids[:, 11]], tbl_12[ids[:, 12]], tbl_13[ids[:, 13]], tbl_14[ids[:, 14]], tbl_15[ids[:, 15]], tbl_16[ids[:, 16]], tbl_17[ids[:, 17]], tbl_18[ids[:, 18]], tbl_19[ids[:, 19]], tbl_20[ids[:, 20]], tbl_21[ids[:, 21]], tbl_22[ids[:, 22]], tbl_23[ids[:, 23]], tbl_24[ids[:, 24]], tbl_25[ids[:, 25]], tbl_26[ids[:, 26]], tbl_27[ids[:, 27]], tbl_28[ids[:, 28]], tbl_29[ids[:, 29]], tbl_30[ids[:, 30]], tbl_31[ids[:, 31]], tbl_32[ids[:, 32]], tbl_33[ids[:, 33]], tbl_34[ids[:, 34]], tbl_35[ids[:, 35]], tbl_36[ids[:, 36]], tbl_37[ids[:, 37]], tbl_38[ids[:, 38]]], axis=1)
    z = _L0_rec_ref(e, L0_rec_f0, L0_rec_f1, L0_rec_f2)
    z = z.reshape(z.shape[0], -1)
    h = jnp.concatenate([z, dense_ctx], axis=1)
    h = jnp.maximum(h @ W_top1 + b_top1, 0.0)
    h = jnp.maximum(h @ W_top2 + b_top2, 0.0)
    y = h @ W_top3
    return y

_drawn_inputs = setup_inputs


def setup_inputs(seed=0):
    import zlib

    import numpy as np

    out = dict(_drawn_inputs(seed))
    spreads = {'b_top1': (0.0, 0.606), 'b_top2': (0.0, 0.277)}
    factors = {'tbl_0': 4.509,
     'tbl_1': 5.386,
     'tbl_2': 4.883,
     'tbl_3': 4.85,
     'tbl_4': 4.601,
     'tbl_5': 5.189,
     'tbl_6': 4.726,
     'tbl_7': 5.001,
     'tbl_8': 4.654,
     'tbl_9': 4.774,
     'tbl_10': 4.887,
     'tbl_11': 4.596,
     'tbl_12': 4.591,
     'tbl_13': 4.516,
     'tbl_14': 4.54,
     'tbl_15': 4.704,
     'tbl_16': 5.168,
     'tbl_17': 4.831,
     'tbl_18': 5.114,
     'tbl_19': 5.088,
     'tbl_20': 4.816,
     'tbl_21': 4.712,
     'tbl_22': 4.611,
     'tbl_23': 4.922,
     'tbl_24': 4.428,
     'tbl_25': 4.716,
     'tbl_26': 4.528,
     'tbl_27': 5.025,
     'tbl_28': 4.306,
     'tbl_29': 4.847,
     'tbl_30': 5.014,
     'tbl_31': 4.45,
     'tbl_32': 5.172,
     'tbl_33': 4.855,
     'tbl_34': 4.718,
     'tbl_35': 4.548,
     'tbl_36': 4.839,
     'tbl_37': 5.321,
     'tbl_38': 4.76,
     'L0_rec_f1': 5.068,
     'L0_rec_f2': 8.0}
    for name, (base, spread) in spreads.items():
        noise = np.random.default_rng([zlib.crc32(name.encode()), seed]).standard_normal(out[name].shape)
        drawn = base * np.exp(spread * noise) if base else spread * noise
        out[name] = jnp.asarray(drawn.astype(out[name].dtype))
    for name, factor in factors.items():
        out[name] = (out[name] * factor).astype(out[name].dtype)
    return out
```

```python
from contextlib import ExitStack

import concourse.bass as bass
from concourse import mybir

F32 = mybir.dt.float32
F32R = mybir.dt.float32r
I32 = mybir.dt.int32
ALU = mybir.AluOpType
ACT = mybir.ActivationFunctionType
AX = mybir.AxisListType

P = 128
F = 39
D = 16
B = 512
M = 128
TB = P // D
NT = B // TB
GT = 4
NG = NT // GT
BT = B // P
SHIFTS = (F + 1) // 2
EXT = F + SHIFTS - 1
JC = 3
KC = JC * F
NC1 = -(-SHIFTS // JC)
KLAST = SHIFTS * F - (NC1 - 1) * KC
ZPAD = NC1 * KC
XA = 4
BANK = 512
FB = BANK // M
NB = -(-F // FB)
RING = 4
ACT_BANKS = (1, 3, 6, 8)
DVE_BANKS = tuple(b for b in range(NB) if b not in ACT_BANKS)
NA = len(ACT_BANKS)
FG = F + 1
AHEAD = 7
DEPTH = 8
H1, H2 = 512, 256
NDENSE = 16


def fields(b):
    return range(b * FB, min(F, (b + 1) * FB))


DVE_PER_TILE = sum(len(fields(b)) for b in DVE_BANKS)


def dve_products_through(b):
    return sum(len(fields(x)) for x in DVE_BANKS if x <= b)


def cin_tower(nc, ids, tables, w0a, w0b, f1, f2, dense_t, w_top1, b_top1, w_top2, b_top2, w_top3,
              consts, scratch, y):
    with ExitStack() as ctx:
        def sb(name, shape, dt=F32):
            return ctx.enter_context(nc.sbuf_tensor(name, shape, dt))

        def ps(name, shape):
            return ctx.enter_context(nc.psum_tensor(name, shape, F32))

        def sem(name):
            return ctx.enter_context(nc.semaphore(name))

        idx = sb("idx", [P, BT, F], I32)
        looked = sb("looked", [P, 2, F, D])
        ext = sb("ext", [P, D, EXT])
        const_sb = sb("const_sb", [P, P + TB])
        identity = const_sb[:, 0:P]
        same_sample = const_sb[:, P:P + TB]
        ws = sb("ws", [KC, NC1, M])
        w1_hi = sb("w1_hi", [P, F * M], F32R)
        w1_lo = sb("w1_lo", [P, F * M], F32R)
        w2 = sb("w2", [P, F, M])
        wt3 = sb("wt3", [P, H2 // P])
        bt1 = sb("bt1", [P, H1 // P])
        bt2 = sb("bt2", [P, H2 // P])
        e_pairs = sb("e_pairs", [P, GT, EXT])
        e_tile = sb("e_tile", [P, GT, EXT])
        pair_prod = sb("pair_prod", [P, 2, ZPAD])
        z = sb("z", [P, NC1, GT * P])
        cur1 = sb("cur1", [P, GT * P])
        cur1_hi = sb("cur1_hi", [P, GT, P], F32R)
        cur1_lo = sb("cur1_lo", [P, GT, P], F32R)
        act_prod = sb("act_prod", [P, NA, BANK])
        act_sum = sb("act_sum", [P, 2, BANK])
        act_fold = sb("act_fold", [P, BANK // 2])
        act_total = sb("act_total", [P, 2, M])
        dve_acc = sb("dve_acc", [P, 2, FB, M])
        dve_fold = sb("dve_fold", [P, FB // 2, M])
        dve_total = sb("dve_total", [P, M])
        cur2 = sb("cur2", [P, 2, M])
        e_block = sb("e_block", [P, 2, FG, TB])
        gram = sb("gram", [P, FG, B])
        w1_raw = gram[:, 0:-(-F * M // B), :].rearrange("p a b -> p (a b)")[:, 0:F * M]
        z1 = sb("z1", [P, B])
        ws_b = gram[0:KC, 32:34, :].rearrange("p a b -> p (a b)")[:, 0:NC1 * M]
        spare = z[:, :, :].rearrange("p c n -> p (c n)")
        wt1 = spare[:, 0:3 * H1].rearrange("p (c n) -> p c n", c=3)
        wt1_dense = spare[0:NDENSE, 3 * H1:4 * H1]
        wt2 = spare[:, 4 * H1:4 * H1 + H1 // P * H2].rearrange("p (c n) -> p c n", n=H2)
        dense = spare[0:NDENSE, 4 * H1 + H1 // P * H2:4 * H1 + H1 // P * H2 + B]
        h1 = act_prod
        h2 = pair_prod[:, :, :].rearrange("p a n -> p (a n)")[:, 0:H2 // P * B].rearrange("p (c n) -> p c n", n=B)
        z3 = act_sum[:, 0, :]
        y_sb = act_sum[0:1, 1, :]

        l2 = [ps(f"l2_{r}", [P, BANK]) for r in range(RING)]
        xp = [ps(f"xp_{r}", [P, BANK]) for r in range(2)]
        l1 = ps("l1", [P, BANK])
        gm = ps("gm", [P, BANK])

        ids_in = sem("ids_in")
        consts_in = sem("consts_in")
        w0_in = sem("w0_in")
        w1_in = sem("w1_in")
        w2_in = sem("w2_in")
        top_in = sem("top_in")
        gathered = [sem(f"gathered_{t}") for t in range(BT)]
        ext_main = sem("ext_main")
        ext_made = sem("ext_made")
        scratch_written = sem("scratch_written")
        e_pairs_in = [sem(f"e_pairs_in_{q}") for q in range(GT)]
        e_tile_in = [sem(f"e_tile_in_{q}") for q in range(GT)]
        pads_zeroed = sem("pads_zeroed")
        ws_made = sem("ws_made")
        w1_hi_made = sem("w1_hi_made")
        w1_lo_made = sem("w1_lo_made")
        block_ones = sem("block_ones")
        pairs_made = sem("pairs_made")
        transposed = sem("transposed")
        z_copied = sem("z_copied")
        layer1_done = sem("layer1_done")
        cur1_copied = sem("cur1_copied")
        z1_made = sem("z1_made")
        hi_made = sem("hi_made")
        lo_made = sem("lo_made")
        layer2_bank = sem("layer2_bank")
        act_products = sem("act_products")
        dve_products = sem("dve_products")
        act_pair_sum = sem("act_pair_sum")
        act_sum_steps = sem("act_sum_steps")
        act_total_made = sem("act_total_made")
        dve_folds = sem("dve_folds")
        cur2_made = sem("cur2_made")
        block_made = sem("block_made")
        gram_done = sem("gram_done")
        gram_copied = sem("gram_copied")
        z3_done = sem("z3_done")
        z3_copied = sem("z3_copied")
        top1_done = sem("top1_done")
        h1_made = sem("h1_made")
        top2_done = sem("top2_done")
        h2_made = sem("h2_made")
        top3_done = sem("top3_done")
        y_copied = sem("y_copied")
        y_out = sem("y_out")

        block = ctx.enter_context(nc.Block())

        def wait(eng, s, value):
            if not (isinstance(value, int) and value <= 0):
                eng.wait_ge(s, value)

        def groups(eng, body):
            first, last = 1, NG - 3
            for i in range(first):
                body(i, lambda n: n < NT)
            with eng.Fori(first, last) as i:
                body(i, lambda n: True)
            for i in range(last, NG):
                body(i, lambda n: n < NT)

        scratch_rows = scratch.rearrange("b (d f) -> (b d) f", f=EXT)

        @block.sync
        def _(sp):
            sp.dma_start(idx[:, :, :], ids.rearrange("(t p) f -> p t f", p=P)).then_inc(ids_in, 16)
            sp.dma_start(w1_raw.rearrange("g (f h) -> g f h", h=M),
                         f1.rearrange("(f g) h -> g f h", g=M)).then_inc(w1_in, 16)
            sp.dma_start(w2[:, :, :], f2.rearrange("(f h) m -> h f m", h=M)).then_inc(w2_in, 16)
            for t in range(BT):
                sp.wait_ge(ext_made, t + 1)
                for g in range(GT):
                    if t or g:
                        sp.wait_ge(scratch_written, 16 * (t * GT + g))
                    b0 = t * P + g * (P // GT)
                    sp.dma_start(scratch[b0:b0 + P // GT, :],
                                 ext[g * (P // GT):(g + 1) * (P // GT), :, :]
                                 .rearrange("p d f -> p (d f)")).then_inc(scratch_written, 16)

            def load_pairs(row, q):
                sp.dma_start(e_pairs[:, q, :], scratch_rows[bass.ds(row, P), :]).then_inc(e_pairs_in[q], 16)

            def load_tile(row, q):
                sp.dma_start(e_tile[:, q, :], scratch_rows[bass.ds(row, P), :]).then_inc(e_tile_in[q], 16)

            sp.wait_ge(scratch_written, 16 * NG)
            for n in range(GT):
                load_pairs(n * P, n)
                load_tile(n * P, n)
            for n in range(GT, DEPTH + GT):
                sp.wait_ge(pairs_made, n - GT + 1)
                load_pairs(n * P, n % GT)

            def body(i, there):
                for q in range(GT):
                    n = i * GT + q
                    if there(n + DEPTH + GT):
                        sp.wait_ge(pairs_made, n + DEPTH + 1)
                        sp.wait_ge(scratch_written, 16 * NG)
                        load_pairs((n + DEPTH + GT) * P, q)
                    if there(n + GT):
                        sp.wait_ge(cur2_made, n + 1)
                        sp.wait_ge(scratch_written, 16 * NG)
                        load_tile((n + GT) * P, q)

            groups(sp, body)
            sp.wait_ge(layer1_done, NG)
            sp.dma_start(wt1, w_top1[0:3 * M, :].rearrange("(c p) n -> p c n", p=P)).then_inc(top_in, 16)
            sp.dma_start(wt1_dense, w_top1[3 * M:, :]).then_inc(top_in, 16)
            sp.dma_start(wt2, w_top2.rearrange("(c p) n -> p c n", p=P)).then_inc(top_in, 16)
            sp.dma_start(dense, dense_t).then_inc(top_in, 16)
            sp.wait_ge(y_copied, 1)
            sp.dma_start(y.rearrange("b o -> o b"), y_sb).then_inc(y_out, 16)
            sp.wait_ge(y_out, 16)

        @block.gpsimd
        def _(pool):
            pool.wait_ge(ids_in, 16)
            for t in range(BT):
                if t >= 2:
                    pool.wait_ge(ext_made, t - 1)
                for f in range(F):
                    nc.gpsimd.indirect_dma_start(
                        out=looked[:, t % 2, f, :], out_offset=None, in_=tables[f],
                        in_offset=bass.IndirectOffsetOnAxis(ap=idx[:, t, f:f + 1], axis=0),
                    ).then_inc(gathered[t], 16)

            def make_pairs(n, par, q, uses):
                pool.wait_ge(e_pairs_in[q], 16 * uses)
                wait(pool, transposed, 2 * (n - 1))
                e = e_pairs[:, q, :]
                a = e[:, 0:F].unsqueeze(1).to_broadcast([P, SHIFTS, F])
                b = bass.AP(e.tensor, e.offset, [list(e.ap[0]), [1, SHIFTS], [1, F]])
                nc.gpsimd.tensor_tensor(
                    pair_prod[:, par, 0:SHIFTS * F].rearrange("p (k f) -> p k f", f=F), a, b,
                    ALU.mult).then_inc(pairs_made, 1)

            pool.wait_ge(pads_zeroed, 1)
            for n in range(DEPTH):
                make_pairs(n, n % 2, n % GT, n // GT + 1)

            def body(i, there):
                for q in range(GT):
                    n = i * GT + q
                    par = q % 2
                    if there(n + DEPTH):
                        make_pairs(n + DEPTH, par, q, i + DEPTH // GT + 1)
                    pool.wait_ge(e_tile_in[q], 16 * (i + 1))
                    wait(pool, gram_done, n - 1)
                    if isinstance(i, int) and n < 2:
                        pool.wait_ge(block_ones, 2)
                    nc.gpsimd.tensor_tensor(
                        e_block[:, par, 0:F, :],
                        e_tile[:, q, 0:F].unsqueeze(2).to_broadcast([P, F, TB]),
                        same_sample.unsqueeze(1).to_broadcast([P, F, TB]),
                        ALU.mult).then_inc(block_made, 1)
                    for half in range(2):
                        pool.wait_ge(act_products, n * NA + 2 * half + 2)
                        wait(pool, act_sum_steps, 2 * n)
                        nc.gpsimd.tensor_tensor(act_sum[:, half, :], act_prod[:, 2 * half, :],
                                                act_prod[:, 2 * half + 1, :], ALU.add).then_inc(act_pair_sum, 1)
                    pool.wait_ge(act_pair_sum, 2 * n + 2)
                    nc.gpsimd.tensor_tensor(act_sum[:, 0, :], act_sum[:, 0, :], act_sum[:, 1, :],
                                            ALU.add).then_inc(act_sum_steps, 1)
                    pool.wait_ge(act_sum_steps, 2 * n + 1)
                    wait(pool, act_total_made, n)
                    nc.gpsimd.tensor_tensor(act_fold[:, :], act_sum[:, 0, 0:BANK // 2],
                                            act_sum[:, 0, BANK // 2:BANK], ALU.add).then_inc(act_sum_steps, 1)
                    pool.wait_ge(act_sum_steps, 2 * n + 2)
                    wait(pool, cur2_made, n - 1)
                    nc.gpsimd.tensor_tensor(act_total[:, par, :], act_fold[:, 0:M], act_fold[:, M:2 * M],
                                            ALU.add).then_inc(act_total_made, 1)

            groups(pool, body)

        @block.scalar
        def _(act):
            act.dma_start(const_sb[:, :], consts).then_inc(consts_in, 16)
            act.dma_start(ws[:, :, :], w0a).then_inc(w0_in, 16)
            act.dma_start(ws_b, w0b.rearrange("p c m -> p (c m)")).then_inc(w0_in, 16)
            act.dma_start(wt3[:, :], w_top3).then_inc(top_in, 16)
            act.dma_start(bt1[:, :], b_top1).then_inc(top_in, 16)
            act.dma_start(bt2[:, :], b_top2).then_inc(top_in, 16)
            act.wait_ge(w1_in, 16)
            nc.scalar.copy(w1_hi[:, :], w1_raw).then_inc(w1_hi_made, 1)

            def copy_z(n, q, group):
                wait(act, layer1_done, group)
                act.wait_ge(transposed, 2 * n + 1)
                nc.scalar.copy(z[0:KC, 0:XA, q * P:(q + 1) * P],
                               xp[0][0:KC, :].rearrange("p (c n) -> p c n", n=P)).then_inc(z_copied, 1)
                act.wait_ge(transposed, 2 * n + 2)
                nc.scalar.copy(z[0:KC, XA:NC1, q * P:(q + 1) * P],
                               xp[1][0:KC, 0:(NC1 - XA) * P].rearrange("p (c n) -> p c n", n=P)).then_inc(z_copied, 1)

            def copy_cur1(group):
                act.wait_ge(layer1_done, group + 1)
                wait(act, lo_made, GT * group)
                wait(act, z1_made, group)
                nc.scalar.copy(cur1[:, :], l1[:, :]).then_inc(cur1_copied, 1)

            act.wait_ge(ws_made, 1)
            for n in range(GT):
                copy_z(n, n, 0)
            copy_cur1(0)
            for n in range(GT, AHEAD):
                copy_z(n, n % GT, n // GT)

            def copy_gram(n):
                act.wait_ge(gram_done, n + 1)
                if isinstance(n, int) and n == 0:
                    act.wait_ge(w1_lo_made, 1)
                nc.scalar.copy(gram[:, :, bass.ds(n * TB, TB)],
                               gm[:, 0:FG * TB].rearrange("p (f b) -> p f b", b=TB)).then_inc(gram_copied, 1)

            def body(i, there):
                for q in range(GT):
                    n = i * GT + q
                    if there(n + AHEAD):
                        copy_z(n + AHEAD, (q + AHEAD) % GT, i + (q + AHEAD) // GT)
                    act.wait_ge(e_tile_in[q], 16 * (i + 1))
                    for r, b in enumerate(ACT_BANKS):
                        act.wait_ge(layer2_bank, n * NB + b + 1)
                        wait(act, act_pair_sum, 2 * n - 2 + r // 2 + 1)
                        for j, f in enumerate(fields(b)):
                            last = nc.scalar.activation(act_prod[:, r, j * M:(j + 1) * M],
                                                        l2[(q * NB + b) % RING][:, j * M:(j + 1) * M],
                                                        ACT.Copy, scale=e_tile[:, q, f:f + 1])
                        last.then_inc(act_products, 1)
                        if r == 1 and q == 1 and there(n + GT):
                            copy_cur1(i + 1)
                    if not (isinstance(n, int) and n == 0):
                        copy_gram(n - 1)

            groups(act, body)
            copy_gram(NT - 1)
            act.wait_ge(z3_done, 1)
            nc.scalar.copy(z3, gm[:, :]).then_inc(z3_copied, 1)
            for c in range(H1 // P):
                act.wait_ge(top1_done, c + 1)
                nc.scalar.activation(h1[:, c, :], l2[c][:, :], ACT.Relu, bias=bt1[:, c:c + 1]).then_inc(h1_made, 1)
            for c in range(H2 // P):
                act.wait_ge(top2_done, c + 1)
                nc.scalar.activation(h2[:, c, :], xp[c][:, :], ACT.Relu, bias=bt2[:, c:c + 1]).then_inc(h2_made, 1)
            act.wait_ge(top3_done, 1)
            nc.scalar.copy(y_sb, l1[0:1, :]).then_inc(y_copied, 1)

        @block.vector
        def _(dve):
            dve.wait_ge(w0_in, 32)
            nc.vector.tensor_tensor(ws[:, :, :].rearrange("p c m -> p (c m)"),
                                    ws[:, :, :].rearrange("p c m -> p (c m)"), ws_b,
                                    ALU.add).then_inc(ws_made, 1)
            nc.vector.memset(pair_prod[:, :, SHIFTS * F:], 0.0).then_inc(pads_zeroed, 1)
            dve.wait_ge(consts_in, 16)
            for par in range(2):
                nc.vector.tensor_copy(e_block[:, par, F, :], same_sample).then_inc(block_ones, 1)
            dve.wait_ge(w1_hi_made, 1)
            nc.vector.tensor_tensor(w1_lo[:, :], w1_raw, w1_hi[:, :].bitcast(F32),
                                    ALU.subtract).then_inc(w1_lo_made, 1)
            for t in range(BT):
                dve.wait_ge(gathered[t], 16 * F)
                if t:
                    dve.wait_ge(scratch_written, 16 * GT * t)
                nc.vector.tensor_copy(ext[:, :, 0:F],
                                      looked[:, t % 2, :, :].rearrange("p f d -> p d f")).then_inc(ext_main, 1)
                nc.vector.tensor_copy(ext[:, :, F:EXT],
                                      looked[:, t % 2, 0:EXT - F, :].rearrange("p f d -> p d f")).then_inc(ext_made, 1)

            def split_hi(n, q, group):
                dve.wait_ge(cur1_copied, group + 1)
                wait(dve, layer2_bank, (n - GT + 1) * NB)
                nc.vector.tensor_copy(cur1_hi[:, q, :], cur1[:, q * P:(q + 1) * P]).then_inc(hi_made, 1)

            def split_lo(n, q):
                dve.wait_ge(hi_made, n + 1)
                nc.vector.tensor_tensor(cur1_lo[:, q, :], cur1[:, q * P:(q + 1) * P],
                                        cur1_hi[:, q, :].bitcast(F32), ALU.subtract).then_inc(lo_made, 1)

            def sum_cur1(group):
                nc.vector.tensor_reduce(z1[:, bass.ts(group, GT * TB)],
                                        cur1[:, :].rearrange("p (b d) -> p b d", d=D),
                                        AX.X, ALU.add).then_inc(z1_made, 1)

            for n in range(GT - 1):
                split_hi(n, n, 0)
                split_lo(n, n)
            sum_cur1(0)

            def fold(n, par, step):
                if step == 0:
                    dve.wait_ge(dve_products, (n + 1) * DVE_PER_TILE)
                    nc.vector.tensor_tensor(dve_fold[:, :, :], dve_acc[:, par, 0:FB // 2, :],
                                            dve_acc[:, par, FB // 2:FB, :], ALU.add).then_inc(dve_folds, 1)
                elif step == 1:
                    dve.wait_ge(dve_folds, 2 * n + 1)
                    nc.vector.tensor_tensor(dve_total[:, :], dve_fold[:, 0, :], dve_fold[:, 1, :],
                                            ALU.add).then_inc(dve_folds, 1)
                else:
                    dve.wait_ge(dve_folds, 2 * n + 2)
                    dve.wait_ge(act_total_made, n + 1)
                    wait(dve, gram_done, n - 1)
                    nc.vector.tensor_tensor(cur2[:, par, :], dve_total[:, :], act_total[:, par, :],
                                            ALU.add).then_inc(cur2_made, 1)

            def body(i, there):
                for q in range(GT):
                    n = i * GT + q
                    par = q % 2
                    dve.wait_ge(e_tile_in[q], 16 * (i + 1))
                    done = 0
                    for r, b in enumerate(DVE_BANKS):
                        dve.wait_ge(layer2_bank, n * NB + b + 1)
                        for j, f in enumerate(fields(b)):
                            acc = dve_acc[:, par, j, :]
                            part = l2[(q * NB + b) % RING][:, j * M:(j + 1) * M]
                            if r == 0:
                                nc.vector.tensor_scalar(acc, part, e_tile[:, q, f:f + 1], None,
                                                        ALU.mult).then_inc(dve_products, 1)
                            else:
                                dve.wait_ge(dve_products, n * DVE_PER_TILE + done - FB + 1)
                                nc.vector.scalar_tensor_tensor(acc, part, e_tile[:, q, f:f + 1], acc,
                                                               ALU.mult, ALU.add).then_inc(dve_products, 1)
                            done += 1
                        if r < 3 and not (isinstance(n, int) and n == 0):
                            fold(n - 1, 1 - par, r)
                        if r == 3 and there(n + GT - 1):
                            split_hi(n + GT - 1, (q + GT - 1) % GT, i + (q + GT - 1) // GT)
                        if r == 4 and there(n + GT - 1):
                            split_lo(n + GT - 1, (q + GT - 1) % GT)
                        if r == 5 and q == 1 and there(n + GT):
                            sum_cur1(i + 1)

            groups(dve, body)
            for step in range(3):
                fold(NT - 1, 1, step)

        @block.tensor
        def _(pe):
            def transpose(n, par):
                pe.wait_ge(pairs_made, n + 1)
                for c in range(NC1):
                    x = c // XA
                    if c % XA == 0:
                        wait(pe, z_copied, 2 * (n - 1) + x + 1)
                    last = nc.tensor.transpose(xp[x][0:KC, (c % XA) * P:(c % XA + 1) * P],
                                               pair_prod[:, par, c * KC:(c + 1) * KC], identity)
                    if c == XA - 1 or c == NC1 - 1:
                        last.then_inc(transposed, 1)

            def layer1(group):
                pe.wait_ge(z_copied, 2 * GT * (group + 1))
                wait(pe, cur1_copied, group)
                for c in range(NC1):
                    k = KC if c < NC1 - 1 else KLAST
                    last = nc.tensor.matmul(l1[:, :], ws[0:k, c, :], z[0:k, c, :],
                                            start=(c == 0), stop=(c == NC1 - 1))
                last.then_inc(layer1_done, 1)

            def gram_tile(n, par):
                pe.wait_ge(cur2_made, n + 1)
                pe.wait_ge(block_made, n + 1)
                wait(pe, gram_copied, n)
                nc.tensor.matmul(gm[:, 0:FG * TB], cur2[:, par, :],
                                 e_block[:, par, :, :].rearrange("p f b -> p (f b)"),
                                 start=True, stop=True).then_inc(gram_done, 1)

            def bank_is_free(n, b):
                dn, b = (0, b - RING) if b >= RING else (-1, b - RING + NB)
                if b in ACT_BANKS:
                    wait(pe, act_products, (n + dn) * NA + ACT_BANKS.index(b) + 1)
                else:
                    wait(pe, dve_products, (n + dn) * DVE_PER_TILE + dve_products_through(b))

            pe.wait_ge(consts_in, 16)
            pe.wait_ge(ws_made, 1)
            for n in range(GT):
                transpose(n, n % 2)
            layer1(0)
            for n in range(GT, AHEAD):
                transpose(n, n % 2)
            pe.wait_ge(w1_lo_made, 1)

            def body(i, there):
                for q in range(GT):
                    n = i * GT + q
                    if there(n + AHEAD):
                        transpose(n + AHEAD, (q + AHEAD) % 2)
                    pe.wait_ge(lo_made, n + 1)
                    for b in range(NB):
                        bank = l2[(q * NB + b) % RING]
                        bank_is_free(n, b)
                        cols = slice(b * BANK, b * BANK + len(fields(b)) * M)
                        out = bank[:, 0:len(fields(b)) * M]
                        nc.tensor.matmul(out, cur1_hi[:, q, :], w1_lo[:, cols], start=True, stop=False)
                        nc.tensor.matmul(out, cur1_lo[:, q, :], w1_hi[:, cols], start=False, stop=False)
                        nc.tensor.matmul(out, cur1_hi[:, q, :], w1_hi[:, cols], start=False,
                                         stop=True).then_inc(layer2_bank, 1)
                        if b == 6 and not (isinstance(n, int) and n == 0):
                            gram_tile(n - 1, 1 - q % 2)
                    if q == 0 and there(n + GT):
                        layer1(i + 1)

            groups(pe, body)
            gram_tile(NT - 1, 1)

            pe.wait_ge(w2_in, 16)
            pe.wait_ge(gram_copied, NT)
            for f in range(F):
                last = nc.tensor.matmul(gm[:, :], w2[:, f, :], gram[:, f, :], start=(f == 0), stop=(f == F - 1))
            last.then_inc(z3_done, 1)
            pe.wait_ge(top_in, 16 * 7)
            pe.wait_ge(z1_made, NG)
            for c in range(H1 // P):
                bank_is_free(NT, c)
                cols = slice(c * P, (c + 1) * P)
                nc.tensor.matmul(l2[c][:, :], wt1[:, 0, cols], z1[:, :], start=True, stop=False)
                nc.tensor.matmul(l2[c][:, :], wt1[:, 1, cols], gram[:, F, :], start=False, stop=False)
                nc.tensor.matmul(l2[c][:, :], wt1_dense[:, cols], dense, start=False, stop=False)
                if c == 0:
                    pe.wait_ge(z3_copied, 1)
                nc.tensor.matmul(l2[c][:, :], wt1[:, 2, cols], z3, start=False,
                                 stop=True).then_inc(top1_done, 1)
            for c in range(H2 // P):
                for k in range(H1 // P):
                    pe.wait_ge(h1_made, k + 1)
                    last = nc.tensor.matmul(xp[c][:, :], wt2[:, k, c * P:(c + 1) * P], h1[:, k, :],
                                            start=(k == 0), stop=(k == H1 // P - 1))
                last.then_inc(top2_done, 1)
            for c in range(H2 // P):
                pe.wait_ge(h2_made, c + 1)
                last = nc.tensor.matmul(l1[0:1, :], wt3[:, c:c + 1], h2[:, c, :], start=(c == 0),
                                        stop=(c == H2 // P - 1))
            last.then_inc(top3_done, 1)


def kernel(**inputs):
    import numpy as np
    import concourse.bacc as bacc
    from concourse.bass_utils import run_bass_kernel_spmd

    nc = bacc.Bacc("TRN2", target_bir_lowering=False, num_devices=1)
    arrays = {}

    def given(name, a):
        a = np.ascontiguousarray(a)
        arrays[name] = a
        return nc.dram_tensor(name, a.shape, mybir.dt.from_np(a.dtype), kind="ExternalInput").ap()

    f0 = np.asarray(inputs["L0_rec_f0"])
    c, j, f = np.meshgrid(np.arange(NC1), np.arange(JC), np.arange(F), indexing="ij")
    k = JC * c + j
    other = (f + k) % F
    padded = np.concatenate([f0, np.zeros((1, M), f0.dtype)])
    one = np.where(k < SHIFTS, f * F + other, F * F).reshape(NC1, KC).T
    two = np.where((k < SHIFTS) & (k > 0), other * F + f, F * F).reshape(NC1, KC).T
    consts = np.concatenate([np.eye(P, dtype=np.float32),
                             np.repeat(np.eye(TB, dtype=np.float32), D, axis=0)], axis=1)
    args = dict(
        ids=given("ids", inputs["ids"]),
        tables=[given(f"tbl_{t}", inputs[f"tbl_{t}"]) for t in range(F)],
        w0a=given("w0a", padded[one]),
        w0b=given("w0b", padded[two]),
        f1=given("f1", inputs["L0_rec_f1"]),
        f2=given("f2", inputs["L0_rec_f2"]),
        dense_t=given("dense_t", np.asarray(inputs["dense_ctx"]).T),
        w_top1=given("w_top1", inputs["W_top1"]),
        b_top1=given("b_top1", np.asarray(inputs["b_top1"]).reshape(H1 // P, P).T),
        w_top2=given("w_top2", inputs["W_top2"]),
        b_top2=given("b_top2", np.asarray(inputs["b_top2"]).reshape(H2 // P, P).T),
        w_top3=given("w_top3", np.asarray(inputs["W_top3"]).reshape(H2 // P, P).T),
        consts=given("consts", consts),
        scratch=nc.dram_tensor("scratch", (B, D * EXT), F32, kind="Internal").ap(),
        y=nc.dram_tensor("y", (B, 1), F32, kind="ExternalOutput").ap(),
    )
    cin_tower(nc, **args)
    r = run_bass_kernel_spmd(nc, [arrays], core_ids=[0])
    return r.results[0]["y"]
```

```python
from contextlib import ExitStack

import concourse.bass as bass
from concourse import mybir

F32 = mybir.dt.float32
F32R = mybir.dt.float32r
I32 = mybir.dt.int32
ALU = mybir.AluOpType
ACT = mybir.ActivationFunctionType
AX = mybir.AxisListType

P = 128
F = 39
D = 16
B = 512
M = 128
TB = P // D
NT = B // TB
GT = 4
NG = NT // GT
BT = B // P
SHIFTS = (F + 1) // 2
EXT = F + SHIFTS - 1
JC = 3
KC = JC * F
NC1 = -(-SHIFTS // JC)
KLAST = SHIFTS * F - (NC1 - 1) * KC
BANK = 512
FB = BANK // M
NB = -(-F // FB)
RING = 4
ACT_BANKS = (1, 2, 4, 5, 7, 8)
POOL_SUMS = 4
DVE_BANKS = tuple(b for b in range(NB) if b not in ACT_BANKS)
NA = len(ACT_BANKS)
DVE_ADDS = NA - POOL_SUMS + 1
FG = F + 1
L1_AHEAD = 2
DEPTH = L1_AHEAD * GT + 1
H1, H2 = 512, 256
NDENSE = 16


BATCH = NT // BT
GATHERS = 3


CHUNK_AT = {(0, 7): 0, (1, 1): 1, (1, 6): 2, (2, 1): 3, (2, 6): 4, (3, 1): 5, (3, 6): 6, (3, 9): 7}
PAIRS_EARLY = (None, 1, 3, 5)
PAIRS_LATE = (0, 2, 4, 6)
GRAM_AFTER = 9
COPY_CUR1 = 4
CLOSE_AFTER = ((0, 1), (2,), (3, 4), ())


def fields(b):
    return range(b * FB, min(F, (b + 1) * FB))


DVE_PER_TILE = sum(len(fields(b)) for b in DVE_BANKS)


def dve_products_through(b):
    return sum(len(fields(x)) for x in DVE_BANKS if x <= b)


def cin_tower(nc, ids, tables, w0a, w0b, f1, f2, dense_t, w_top1, b_top1, w_top2, b_top2, w_top3,
              consts, scratch, y):
    with ExitStack() as ctx:
        def sb(name, shape, dt=F32):
            return ctx.enter_context(nc.sbuf_tensor(name, shape, dt))

        def ps(name, shape):
            return ctx.enter_context(nc.psum_tensor(name, shape, F32))

        def sem(name):
            return ctx.enter_context(nc.semaphore(name))

        idx = sb("idx", [P, BT, F], I32)
        one = sb("one", [P, 1])
        idx_batch = sb("idx_batch", [P, F], I32)
        looked = sb("looked", [P, F, D])
        ext = sb("ext", [P, D, EXT])
        const_sb = sb("const_sb", [P, P + TB])
        identity = const_sb[:, 0:P]
        same_sample = const_sb[:, P:P + TB]
        ws = sb("ws", [KC, NC1, M])
        w1_hi = sb("w1_hi", [P, F * M], F32R)
        w1_lo = sb("w1_lo", [P, F * M], F32R)
        w2 = sb("w2", [P, F, M])
        wt3 = sb("wt3", [P, H2 // P])
        bt1 = sb("bt1", [P, H1 // P])
        bt2 = sb("bt2", [P, H2 // P])
        e_pairs = sb("e_pairs", [P, GT, EXT])
        e_tile = sb("e_tile", [P, GT, EXT])
        pair_prod = sb("pair_prod", [P, 2, GT, KC])
        z = sb("z", [KC, 2, GT * P])
        cur1 = sb("cur1", [P, GT * P])
        cur1_hi = sb("cur1_hi", [P, GT, P], F32R)
        cur1_lo = sb("cur1_lo", [P, GT, P], F32R)
        act_prod = sb("act_prod", [P, NA, BANK])
        act_sum = sb("act_sum", [P, BANK])
        pool_sum = sb("pool_sum", [P, 2, BANK])
        dve_acc = sb("dve_acc", [P, 2, FB, M])
        dve_fold = sb("dve_fold", [P, FB // 2, M])
        cur2 = sb("cur2", [P, 2, M])
        e_block = sb("e_block", [P, 2, FG, TB])
        gram = sb("gram", [P, FG, B])
        w1_raw = gram[:, 0:-(-F * M // B), :].rearrange("p a b -> p (a b)")[:, 0:F * M]
        z1 = sb("z1", [P, B])
        ws_b = gram[0:KC, 32:34, :].rearrange("p a b -> p (a b)")[:, 0:NC1 * M]
        wt1 = sb("wt1", [P, 3, H1])
        wt1_dense = sb("wt1_dense", [NDENSE, H1])
        wt2 = sb("wt2", [P, H1 // P, H2])
        dense = sb("dense", [NDENSE, B])
        h1 = act_prod[:, 0:H1 // P, :]
        h2 = dve_acc[:, :, :, :].rearrange("p c j m -> p c (j m)")
        z3 = act_sum
        y_sb = pool_sum[0:1, 0, :]

        l2 = [ps(f"l2_{r}", [P, BANK]) for r in range(RING)]
        xp = [ps(f"xp_{r}", [P, BANK]) for r in range(2)]
        l1 = ps("l1", [P, BANK])
        gm = ps("gm", [P, BANK])

        ids_in = sem("ids_in")
        consts_in = sem("consts_in")
        w0_in = sem("w0_in")
        w1_in = sem("w1_in")
        w2_in = sem("w2_in")
        top_in = sem("top_in")
        one_made = sem("one_made")
        idx_copied = sem("idx_copied")
        gathered = sem("gathered")
        ext_main = sem("ext_main")
        ext_made = sem("ext_made")
        scratch_written = sem("scratch_written")
        e_pairs_in = sem("e_pairs_in")
        e_tile_in = [sem(f"e_tile_in_{q}") for q in range(GT)]
        ws_made = sem("ws_made")
        w1_hi_made = sem("w1_hi_made")
        w1_lo_made = sem("w1_lo_made")
        block_ones = sem("block_ones")
        pairs_made = sem("pairs_made")
        transposed = sem("transposed")
        z_copied = sem("z_copied")
        layer1_chunks = sem("layer1_chunks")
        cur1_copied = sem("cur1_copied")
        z1_made = sem("z1_made")
        hi_made = sem("hi_made")
        lo_made = sem("lo_made")
        layer2_bank = sem("layer2_bank")
        act_products = sem("act_products")
        dve_products = sem("dve_products")
        pool_adds = sem("pool_adds")
        dve_adds = sem("dve_adds")
        dve_folds = sem("dve_folds")
        cur2_made = sem("cur2_made")
        block_made = sem("block_made")
        gram_done = sem("gram_done")
        gram_copied = sem("gram_copied")
        z3_done = sem("z3_done")
        z3_copied = sem("z3_copied")
        top1_done = sem("top1_done")
        h1_made = sem("h1_made")
        top2_done = sem("top2_done")
        h2_made = sem("h2_made")
        top3_done = sem("top3_done")
        y_copied = sem("y_copied")
        y_out = sem("y_out")

        block = ctx.enter_context(nc.Block())

        def wait(eng, s, value):
            if not (isinstance(value, int) and value <= 0):
                eng.wait_ge(s, value)

        def groups(eng, body):
            first, last = 1, NG - 3
            for i in range(first):
                body(i, lambda n: n < NT)
            with eng.Fori(first, last) as i:
                body(i, lambda n: True)
            for i in range(last, NG):
                body(i, lambda n: n < NT)

        def slots_before(group, c):
            return group * NC1 + (c - 1 if c >= 2 else -1 if c == 1 else 0)

        def chunk_shifts(c):
            return min(JC, SHIFTS - c * JC)

        def wait_then(eng, s, value):
            eng.wait_ge(ids_in, 16)
            wait(eng, s, value)

        def batches(eng, body):
            for m in range(BATCH):
                body(m, m, 0)
            with eng.Fori(1, BT - 1) as t:
                for s in range(BATCH):
                    body(t * BATCH + s, s, t)
            for m in range((BT - 1) * BATCH, NT + DEPTH):
                body(m, m % BATCH, BT - 1)

        def make_pairs(eng, product, group, c):
            if c == 0:
                eng.wait_ge(e_pairs_in, 16 * (group + 1))
            wait(eng, transposed, slots_before(group, c))
            kc = chunk_shifts(c)
            e = e_pairs[:, :, :]
            row = list(e.ap[0])
            product(pair_prod[:, c % 2, :, 0:kc * F].rearrange("p t (k f) -> p t k f", f=F),
                    bass.AP(e.tensor, e.offset, [row, [EXT, GT], [0, kc], [1, F]]),
                    bass.AP(e.tensor, e.offset + c * JC, [row, [EXT, GT], [1, kc], [1, F]]),
                    ALU.mult).then_inc(pairs_made, 1)

        scratch_rows = scratch.rearrange("b (d f) -> (b d) f", f=EXT)

        @block.sync
        def _(sp):
            sp.dma_start(idx[:, :, :], ids.rearrange("(t p) f -> p t f", p=P)).then_inc(ids_in, 16)
            sp.dma_start(w1_raw.rearrange("g (f h) -> g f h", h=M),
                         f1.rearrange("(f g) h -> g f h", g=M)).then_inc(w1_in, 16)
            sp.dma_start(w2[:, :, :], f2.rearrange("(f h) m -> h f m", h=M)).then_inc(w2_in, 16)

            def write_batch(t):
                wait_then(sp, ext_made, t + 1)
                sp.dma_start(scratch[bass.ds(t * P, P), :],
                             ext[:, :, :].rearrange("p d f -> p (d f)")).then_inc(scratch_written, 16)

            group_rows = scratch_rows.rearrange("(g t p) f -> g p t f", t=GT, p=P)

            def load_pairs(group):
                sp.dma_start(e_pairs[:, :, :], group_rows[bass.ds(group, 1), :, :, :]
                             .rearrange("a p t f -> (a p) t f")).then_inc(e_pairs_in, 16)

            def load_tile(n, q):
                sp.dma_start(e_tile[:, q, :], scratch_rows[bass.ds(n * P, P), :]).then_inc(e_tile_in[q], 16)

            def loads(m, s, batch):
                n = m - DEPTH
                if not isinstance(m, int) or 0 <= n < NT - GT:
                    wait_then(sp, cur2_made, n + 1)
                    load_tile(n + GT, (s - DEPTH) % GT)
                if s % GT == GT - 1 and (not isinstance(m, int) or m < NT - GT):
                    if s == BATCH - 1:
                        write_batch(batch + 1)
                        sp.wait_ge(scratch_written, 16 * (batch + 2))
                    group = batch * (BATCH // GT) + s // GT + 1
                    wait_then(sp, pairs_made, group * NC1)
                    load_pairs(group)

            write_batch(0)
            sp.wait_ge(scratch_written, 16)
            load_pairs(0)
            for n in range(GT):
                load_tile(n, n)
            batches(sp, loads)
            sp.wait_ge(y_copied, 1)
            sp.dma_start(y.rearrange("b o -> o b"), y_sb).then_inc(y_out, 16)
            sp.wait_ge(y_out, 16)

        @block.gpsimd
        def _(pool):
            pool.wait_ge(ids_in, 16)

            def take_indices(t):
                wait_then(pool, ext_made, t)
                nc.gpsimd.tensor_copy(idx_batch[:, :], idx[:, bass.ds(t, 1), :]
                                      .rearrange("p a f -> p (a f)")).then_inc(idx_copied, 1)
                pool.wait_ge(idx_copied, t + 1)

            def gather(f):
                nc.gpsimd.indirect_dma_start(
                    out=looked[:, f, :], out_offset=None, in_=tables[f],
                    in_offset=bass.IndirectOffsetOnAxis(ap=idx_batch[:, f:f + 1], axis=0),
                ).then_inc(gathered, 16)

            def extend(t):
                pool.wait_ge(gathered, (t + 1) * 16 * F)
                wait(pool, scratch_written, t * 16)
                for made, cols, n in ((ext_main, slice(0, F), F), (ext_made, slice(F, EXT), EXT - F)):
                    if made is ext_made:
                        pool.wait_ge(ext_main, t + 1)
                    nc.gpsimd.tensor_tensor(ext[:, :, cols], looked[:, 0:n, :].rearrange("p f d -> p d f"),
                                            one[:, :].unsqueeze(2).to_broadcast([P, D, n]),
                                            ALU.mult).then_inc(made, 1)

            def make_block(n, par, q, uses):
                pool.wait_ge(e_tile_in[q], 16 * uses)
                wait(pool, gram_done, n - 1)
                if isinstance(n, int) and n < 2:
                    pool.wait_ge(block_ones, 2)
                nc.gpsimd.tensor_tensor(
                    e_block[:, par, 0:F, :],
                    e_tile[:, q, 0:F].unsqueeze(2).to_broadcast([P, F, TB]),
                    same_sample.unsqueeze(1).to_broadcast([P, F, TB]),
                    ALU.mult).then_inc(block_made, 1)

            def sum_act(n, par, a):
                adds = POOL_SUMS - 1
                pool.wait_ge(act_products, n * NA + a + 2)
                wait(pool, pool_adds, n * adds + a)
                if a == adds - 1:
                    wait(pool, dve_adds, (n - 1) * DVE_ADDS)
                nc.gpsimd.tensor_tensor(pool_sum[:, par, :] if a == adds - 1 else act_sum[:, :],
                                        act_sum[:, :] if a else act_prod[:, 0, :],
                                        act_prod[:, a + 1, :], ALU.add).then_inc(pool_adds, 1)

            take_indices(0)
            nc.gpsimd.memset(one[:, :], 1.0).then_inc(one_made, 1)
            for f in range(F):
                gather(f)
            pool.wait_ge(one_made, 1)

            def body(m, s, batch):
                n = m - DEPTH
                real = not isinstance(m, int)
                more = real or batch < BT - 1
                if more and s == 0:
                    take_indices(batch + 1)
                gathers = list(range(s * GATHERS, min(F, (s + 1) * GATHERS))) if more else []
                if more and s == BATCH - 2:
                    extend(batch + 1)
                if real or n >= 0:
                    uses = batch * (BATCH // GT) + (s - DEPTH) // GT + 1
                    if not real and m >= NT:
                        uses += BATCH // GT
                    par, q = (s - DEPTH) % 2, (s - DEPTH) % GT
                    make_block(n, par, q, uses)
                if gathers:
                    gather(gathers.pop(0))
                group = batch * (BATCH // GT) + s // GT
                pairs = real or L1_AHEAD * GT <= m < NT
                if pairs and PAIRS_EARLY[s % GT] is not None:
                    make_pairs(pool, nc.gpsimd.tensor_tensor, group, PAIRS_EARLY[s % GT])
                if real or n >= 0:
                    for a in range(POOL_SUMS - 1):
                        sum_act(n, par, a)
                        if gathers:
                            gather(gathers.pop(0))
                for f in gathers:
                    gather(f)
                if pairs:
                    make_pairs(pool, nc.gpsimd.tensor_tensor, group, PAIRS_LATE[s % GT])

            batches(pool, body)

        @block.scalar
        def _(act):
            act.dma_start(const_sb[:, :], consts).then_inc(consts_in, 16)
            act.dma_start(ws[:, :, :], w0a).then_inc(w0_in, 16)
            act.dma_start(ws_b, w0b.rearrange("p c m -> p (c m)")).then_inc(w0_in, 16)
            act.dma_start(wt1[:, :, :], w_top1[0:3 * M, :].rearrange("(c p) n -> p c n", p=P)).then_inc(top_in, 16)
            act.dma_start(wt1_dense[:, :], w_top1[3 * M:, :]).then_inc(top_in, 16)
            act.dma_start(wt2[:, :, :], w_top2.rearrange("(c p) n -> p c n", p=P)).then_inc(top_in, 16)
            act.dma_start(dense[:, :], dense_t).then_inc(top_in, 16)
            act.dma_start(wt3[:, :], w_top3).then_inc(top_in, 16)
            act.dma_start(bt1[:, :], b_top1).then_inc(top_in, 16)
            act.dma_start(bt2[:, :], b_top2).then_inc(top_in, 16)
            act.wait_ge(w1_in, 16)
            nc.scalar.copy(w1_hi[:, :], w1_raw).then_inc(w1_hi_made, 1)

            def copy_z(group, c):
                wait(act, layer1_chunks, slots_before(group, c))
                act.wait_ge(transposed, group * NC1 + c + 1)
                k = chunk_shifts(c) * F
                nc.scalar.copy(z[0:k, c % 2, :], xp[c % 2][0:k, :]).then_inc(z_copied, 1)

            def copy_cur1(group):
                act.wait_ge(layer1_chunks, (group + 1) * NC1)
                wait(act, lo_made, GT * group)
                wait(act, z1_made, group)
                nc.scalar.copy(cur1[:, :], l1[:, :]).then_inc(cur1_copied, 1)

            for c in range(NC1):
                copy_z(0, c)
            copy_cur1(0)
            def copy_gram(n):
                act.wait_ge(gram_done, n + 1)
                if isinstance(n, int) and n == 0:
                    act.wait_ge(w1_lo_made, 1)
                nc.scalar.copy(gram[:, :, bass.ds(n * TB, TB)],
                               gm[:, 0:FG * TB].rearrange("p (f b) -> p f b", b=TB)).then_inc(gram_copied, 1)

            def body(i, there):
                for q in range(GT):
                    n = i * GT + q
                    act.wait_ge(e_tile_in[q], 16 * (i + 1))
                    first = isinstance(n, int) and n == 0
                    second_group = list(range(NC1)) if first else []
                    for r, b in enumerate(ACT_BANKS):
                        while second_group and second_group[0] < b:
                            copy_z(1, second_group.pop(0))
                        act.wait_ge(layer2_bank, n * NB + b + 1)
                        if r < POOL_SUMS:
                            wait(act, pool_adds, (n - 1) * (POOL_SUMS - 1) + max(r, 1))
                        else:
                            wait(act, dve_adds, (n - 1) * DVE_ADDS + r - POOL_SUMS + 1)
                        for j, f in enumerate(fields(b)):
                            last = nc.scalar.activation(act_prod[:, r, j * M:(j + 1) * M],
                                                        l2[(q * NB + b) % RING][:, j * M:(j + 1) * M],
                                                        ACT.Copy, scale=e_tile[:, q, f:f + 1])
                        last.then_inc(act_products, 1)
                        if r == (NA - 1 if first else COPY_CUR1) and q == 0 and there(n + GT):
                            copy_cur1(i + 1)
                        for at, c in CHUNK_AT.items():
                            if (c < NC1 and at[0] == q and (r == 0 or at[1] > ACT_BANKS[r - 1])
                                    and at[1] <= b and there(n + L1_AHEAD * GT)):
                                copy_z(i + L1_AHEAD, c)
                    if not (isinstance(n, int) and n == 0):
                        copy_gram(n - 1)

            groups(act, body)
            copy_gram(NT - 1)
            act.wait_ge(z3_done, 1)
            nc.scalar.copy(z3[:, :], gm[:, :]).then_inc(z3_copied, 1)
            for c in range(H1 // P):
                act.wait_ge(top1_done, c + 1)
                nc.scalar.activation(h1[:, c, :], l2[c][:, :], ACT.Relu, bias=bt1[:, c:c + 1]).then_inc(h1_made, 1)
            for c in range(H2 // P):
                act.wait_ge(top2_done, c + 1)
                nc.scalar.activation(h2[:, c, :], xp[c][:, :], ACT.Relu, bias=bt2[:, c:c + 1]).then_inc(h2_made, 1)
            act.wait_ge(top3_done, 1)
            nc.scalar.copy(y_sb, l1[0:1, :]).then_inc(y_copied, 1)

        @block.vector
        def _(dve):
            dve.wait_ge(w0_in, 32)
            nc.vector.tensor_tensor(ws[:, :, :].rearrange("p c m -> p (c m)"),
                                    ws[:, :, :].rearrange("p c m -> p (c m)"), ws_b,
                                    ALU.add).then_inc(ws_made, 1)
            dve.wait_ge(consts_in, 16)
            for par in range(2):
                nc.vector.tensor_copy(e_block[:, par, F, :], same_sample).then_inc(block_ones, 1)
            dve.wait_ge(w1_hi_made, 1)
            nc.vector.tensor_tensor(w1_lo[:, :], w1_raw, w1_hi[:, :].bitcast(F32),
                                    ALU.subtract).then_inc(w1_lo_made, 1)
            def split_hi(n, q, group):
                dve.wait_ge(cur1_copied, group + 1)
                wait(dve, layer2_bank, (n - GT + 1) * NB)
                nc.vector.tensor_copy(cur1_hi[:, q, :], cur1[:, q * P:(q + 1) * P]).then_inc(hi_made, 1)

            def split_lo(n, q):
                dve.wait_ge(hi_made, n + 1)
                nc.vector.tensor_tensor(cur1_lo[:, q, :], cur1[:, q * P:(q + 1) * P],
                                        cur1_hi[:, q, :].bitcast(F32), ALU.subtract).then_inc(lo_made, 1)

            def sum_cur1(group):
                nc.vector.tensor_reduce(z1[:, bass.ts(group, GT * TB)],
                                        cur1[:, :].rearrange("p (b d) -> p b d", d=D),
                                        AX.X, ALU.add).then_inc(z1_made, 1)

            dve.wait_ge(gathered, 16 * F)
            nc.vector.tensor_copy(ext[:, :, 0:F], looked[:, :, :].rearrange("p f d -> p d f")).then_inc(ext_main, 1)
            dve.wait_ge(ext_main, 1)
            nc.vector.tensor_copy(ext[:, :, F:EXT], looked[:, 0:EXT - F, :]
                                  .rearrange("p f d -> p d f")).then_inc(ext_made, 1)
            for c in range(NC1):
                make_pairs(dve, nc.vector.tensor_tensor, 0, c)
            for c in range(2):
                make_pairs(dve, nc.vector.tensor_tensor, 1, c)
            for n in range(GT - 1):
                split_hi(n, n, 0)
                split_lo(n, n)
            sum_cur1(0)

            def add_banks(n, par, r, share):
                if r == 0:
                    dve.wait_ge(dve_products, (n + 1) * DVE_PER_TILE)
                else:
                    dve.wait_ge(dve_adds, n * DVE_ADDS + r)
                acc = dve_acc[:, par, :, :].rearrange("p j m -> p (j m)")
                nc.vector.tensor_tensor(acc, acc, share, ALU.add).then_inc(dve_adds, 1)

            def close(n, par, step):
                if step < NA - POOL_SUMS:
                    dve.wait_ge(act_products, n * NA + POOL_SUMS + step + 1)
                    add_banks(n, par, step, act_prod[:, POOL_SUMS + step, :])
                elif step == DVE_ADDS - 1:
                    dve.wait_ge(pool_adds, (n + 1) * (POOL_SUMS - 1))
                    add_banks(n, par, step, pool_sum[:, par, :])
                elif step == DVE_ADDS:
                    dve.wait_ge(dve_adds, (n + 1) * DVE_ADDS)
                    nc.vector.tensor_tensor(dve_fold[:, :, :], dve_acc[:, par, 0:FB // 2, :],
                                            dve_acc[:, par, FB // 2:FB, :], ALU.add).then_inc(dve_folds, 1)
                elif step == DVE_ADDS + 1:
                    dve.wait_ge(dve_folds, n + 1)
                    wait(dve, gram_done, n - 1)
                    nc.vector.tensor_tensor(cur2[:, par, :], dve_fold[:, 0, :], dve_fold[:, 1, :],
                                            ALU.add).then_inc(cur2_made, 1)

            def body(i, there):
                for q in range(GT):
                    n = i * GT + q
                    par = q % 2
                    dve.wait_ge(e_tile_in[q], 16 * (i + 1))
                    done = 0
                    second_group = list(range(2, NC1)) if isinstance(n, int) and n == 0 else []
                    for r, b in enumerate(DVE_BANKS):
                        while second_group and second_group[0] <= b + 1:
                            make_pairs(dve, nc.vector.tensor_tensor, 1, second_group.pop(0))
                        dve.wait_ge(layer2_bank, n * NB + b + 1)
                        for j, f in enumerate(fields(b)):
                            acc = dve_acc[:, par, j, :]
                            part = l2[(q * NB + b) % RING][:, j * M:(j + 1) * M]
                            if r == 0:
                                nc.vector.tensor_scalar(acc, part, e_tile[:, q, f:f + 1], None,
                                                        ALU.mult).then_inc(dve_products, 1)
                            else:
                                dve.wait_ge(dve_products, n * DVE_PER_TILE + done - FB + 1)
                                nc.vector.scalar_tensor_tensor(acc, part, e_tile[:, q, f:f + 1], acc,
                                                               ALU.mult, ALU.add).then_inc(dve_products, 1)
                            done += 1
                        if not (isinstance(n, int) and n == 0):
                            for step in CLOSE_AFTER[r]:
                                close(n - 1, 1 - par, step)
                        if r == 1 and there(n + GT - 1):
                            split_hi(n + GT - 1, (q + GT - 1) % GT, i + (q + GT - 1) // GT)
                        if r == 2 and there(n + GT - 1):
                            split_lo(n + GT - 1, (q + GT - 1) % GT)
                        if r == 3 and q == 1 and there(n + GT):
                            sum_cur1(i + 1)

            groups(dve, body)
            for step in range(DVE_ADDS + 2):
                close(NT - 1, 1, step)

        @block.tensor
        def _(pe):
            def transpose(group, c):
                pe.wait_ge(pairs_made, group * NC1 + c + 1)
                wait(pe, z_copied, slots_before(group, c))
                k = chunk_shifts(c) * F
                for t in range(GT):
                    last = nc.tensor.transpose(xp[c % 2][0:k, t * P:(t + 1) * P],
                                               pair_prod[:, c % 2, t, 0:k], identity)
                last.then_inc(transposed, 1)

            def layer1(group, c):
                if c == 0:
                    wait(pe, cur1_copied, group)
                pe.wait_ge(z_copied, group * NC1 + c + 1)
                k = chunk_shifts(c) * F
                nc.tensor.matmul(l1[:, :], ws[0:k, c, :], z[0:k, c % 2, :], start=(c == 0),
                                 stop=(c == NC1 - 1)).then_inc(layer1_chunks, 1)

            def chunk_step(group, c):
                if c < NC1:
                    transpose(group, c)
                if c > 0:
                    layer1(group, c - 1)

            def gram_tile(n, par):
                pe.wait_ge(cur2_made, n + 1)
                pe.wait_ge(block_made, n + 1)
                wait(pe, gram_copied, n)
                nc.tensor.matmul(gm[:, 0:FG * TB], cur2[:, par, :],
                                 e_block[:, par, :, :].rearrange("p f b -> p (f b)"),
                                 start=True, stop=True).then_inc(gram_done, 1)

            def bank_is_free(n, b):
                dn, b = (0, b - RING) if b >= RING else (-1, b - RING + NB)
                if b in ACT_BANKS:
                    wait(pe, act_products, (n + dn) * NA + ACT_BANKS.index(b) + 1)
                else:
                    wait(pe, dve_products, (n + dn) * DVE_PER_TILE + dve_products_through(b))

            pe.wait_ge(consts_in, 16)
            pe.wait_ge(ws_made, 1)
            for c in range(NC1 + 1):
                chunk_step(0, c)
            pe.wait_ge(w1_lo_made, 1)

            def body(i, there):
                for q in range(GT):
                    n = i * GT + q
                    pe.wait_ge(lo_made, n + 1)
                    for b in range(NB):
                        bank = l2[(q * NB + b) % RING]
                        bank_is_free(n, b)
                        cols = slice(b * BANK, b * BANK + len(fields(b)) * M)
                        out = bank[:, 0:len(fields(b)) * M]
                        nc.tensor.matmul(out, cur1_hi[:, q, :], w1_lo[:, cols], start=True, stop=False)
                        nc.tensor.matmul(out, cur1_lo[:, q, :], w1_hi[:, cols], start=False, stop=False)
                        nc.tensor.matmul(out, cur1_hi[:, q, :], w1_hi[:, cols], start=False,
                                         stop=True).then_inc(layer2_bank, 1)
                        if b == GRAM_AFTER and not (isinstance(n, int) and n == 0):
                            gram_tile(n - 1, 1 - q % 2)
                        if isinstance(n, int) and n == 0 and b <= NC1:
                            chunk_step(1, b)
                        if (q, b) in CHUNK_AT and there(n + L1_AHEAD * GT):
                            chunk_step(i + L1_AHEAD, CHUNK_AT[q, b])

            groups(pe, body)
            gram_tile(NT - 1, 1)

            pe.wait_ge(w2_in, 16)
            pe.wait_ge(gram_copied, NT)
            for f in range(F):
                last = nc.tensor.matmul(gm[:, :], w2[:, f, :], gram[:, f, :], start=(f == 0), stop=(f == F - 1))
            last.then_inc(z3_done, 1)
            pe.wait_ge(top_in, 16 * 7)
            pe.wait_ge(z1_made, NG)
            for c in range(H1 // P):
                bank_is_free(NT, c)
                cols = slice(c * P, (c + 1) * P)
                nc.tensor.matmul(l2[c][:, :], wt1[:, 0, cols], z1[:, :], start=True, stop=False)
                nc.tensor.matmul(l2[c][:, :], wt1[:, 1, cols], gram[:, F, :], start=False, stop=False)
                nc.tensor.matmul(l2[c][:, :], wt1_dense[:, cols], dense[:, :], start=False, stop=False)
                if c == 0:
                    pe.wait_ge(z3_copied, 1)
                nc.tensor.matmul(l2[c][:, :], wt1[:, 2, cols], z3[:, :], start=False,
                                 stop=True).then_inc(top1_done, 1)
            for c in range(H2 // P):
                for k in range(H1 // P):
                    pe.wait_ge(h1_made, k + 1)
                    last = nc.tensor.matmul(xp[c][:, :], wt2[:, k, c * P:(c + 1) * P], h1[:, k, :],
                                            start=(k == 0), stop=(k == H1 // P - 1))
                last.then_inc(top2_done, 1)
            for c in range(H2 // P):
                pe.wait_ge(h2_made, c + 1)
                last = nc.tensor.matmul(l1[0:1, :], wt3[:, c:c + 1], h2[:, c, :], start=(c == 0),
                                        stop=(c == H2 // P - 1))
            last.then_inc(top3_done, 1)


def kernel(**inputs):
    import numpy as np
    import concourse.bacc as bacc
    from concourse.bass_utils import run_bass_kernel_spmd

    nc = bacc.Bacc("TRN2", target_bir_lowering=False, num_devices=1)
    arrays = {}

    def given(name, a):
        a = np.ascontiguousarray(a)
        arrays[name] = a
        return nc.dram_tensor(name, a.shape, mybir.dt.from_np(a.dtype), kind="ExternalInput").ap()

    f0 = np.asarray(inputs["L0_rec_f0"])
    c, j, f = np.meshgrid(np.arange(NC1), np.arange(JC), np.arange(F), indexing="ij")
    k = JC * c + j
    other = (f + k) % F
    padded = np.concatenate([f0, np.zeros((1, M), f0.dtype)])
    one = np.where(k < SHIFTS, f * F + other, F * F).reshape(NC1, KC).T
    two = np.where((k < SHIFTS) & (k > 0), other * F + f, F * F).reshape(NC1, KC).T
    consts = np.concatenate([np.eye(P, dtype=np.float32),
                             np.repeat(np.eye(TB, dtype=np.float32), D, axis=0)], axis=1)
    args = dict(
        ids=given("ids", inputs["ids"]),
        tables=[given(f"tbl_{t}", inputs[f"tbl_{t}"]) for t in range(F)],
        w0a=given("w0a", padded[one]),
        w0b=given("w0b", padded[two]),
        f1=given("f1", inputs["L0_rec_f1"]),
        f2=given("f2", inputs["L0_rec_f2"]),
        dense_t=given("dense_t", np.asarray(inputs["dense_ctx"]).T),
        w_top1=given("w_top1", inputs["W_top1"]),
        b_top1=given("b_top1", np.asarray(inputs["b_top1"]).reshape(H1 // P, P).T),
        w_top2=given("w_top2", inputs["W_top2"]),
        b_top2=given("b_top2", np.asarray(inputs["b_top2"]).reshape(H2 // P, P).T),
        w_top3=given("w_top3", np.asarray(inputs["W_top3"]).reshape(H2 // P, P).T),
        consts=given("consts", consts),
        scratch=nc.dram_tensor("scratch", (B, D * EXT), F32, kind="Internal").ap(),
        y=nc.dram_tensor("y", (B, 1), F32, kind="ExternalOutput").ap(),
    )
    cin_tower(nc, **args)
    r = run_bass_kernel_spmd(nc, [arrays], core_ids=[0])
    return r.results[0]["y"]
```

```python
from contextlib import ExitStack

import concourse.bass as bass
from concourse import mybir

F32 = mybir.dt.float32
F32R = mybir.dt.float32r
I32 = mybir.dt.int32
ALU = mybir.AluOpType
ACT = mybir.ActivationFunctionType
AX = mybir.AxisListType

P = 128
F = 39
D = 16
B = 512
M = 128
TB = P // D
NT = B // TB
GT = 4
NG = NT // GT
BT = B // P
SHIFTS = (F + 1) // 2
EXT = F + SHIFTS - 1
JC = 3
KC = JC * F
NC1 = -(-SHIFTS // JC)
BANK = 512
FB = BANK // M
NB = -(-F // FB)
RING = 4
ACT_BANKS = (1, 2, 4, 5, 7, 8)
POOL_SUMS = 4
DVE_BANKS = tuple(b for b in range(NB) if b not in ACT_BANKS)
NA = len(ACT_BANKS)
DVE_ADDS = NA - POOL_SUMS + 1
FG = F + 1
L1_AHEAD = 2
DEPTH = L1_AHEAD * GT + 1
SPLIT_FIELDS = 8
W2_CHUNKS = [slice(f * M, min(F, f + SPLIT_FIELDS) * M) for f in range(0, F, SPLIT_FIELDS)]
H1, H2 = 512, 256
NDENSE = 16
BATCH = NT // BT
GATHERS = 3

TRANSPOSE_AT = {(0, 3): 0, (0, 8): 1, (1, 3): 2, (1, 8): 3, (2, 3): 4, (2, 8): 5, (3, 3): 6}
LAYER1_AT = {(1, 1): 0, (1, 6): 1, (2, 1): 2, (2, 6): 3, (3, 1): 4, (3, 6): 5, (3, 9): 6}
TRANSPOSE_AT_FIRST = {(0, 8): 0, (1, 1): 1, (1, 6): 2, (2, 1): 3, (2, 6): 4, (3, 1): 5, (3, 4): 6}
LAYER1_AT_FIRST = {(1, 3): 0, (1, 8): 1, (2, 3): 2, (2, 8): 3, (3, 2): 4, (3, 6): 5, (3, 9): 6}
PAIRS_EARLY = (None, 1, 3, 5)
PAIRS_LATE = (0, 2, 4, 6)
GRAM_LAG = 2
GRAM_AFTER = 0
GRAM_COPY = ACT_BANKS[0]
BLOCK_RANK = 3
COPY_CUR1 = 4
CLOSE_AFTER = ((0, 1), (2,), (3, 4), ())


def fields(b):
    return range(b * FB, min(F, (b + 1) * FB))


def chunks_beside(group):
    first = isinstance(group, int) and group == 0
    return (TRANSPOSE_AT_FIRST, LAYER1_AT_FIRST) if first else (TRANSPOSE_AT, LAYER1_AT)


def split_after(tile, bank):
    later = [b for b in DVE_BANKS if b >= bank + 2]
    return (tile, later[0]) if later else (tile + 1, DVE_BANKS[0])


DVE_PER_TILE = sum(len(fields(b)) for b in DVE_BANKS)


def dve_products_through(b):
    return sum(len(fields(x)) for x in DVE_BANKS if x <= b)


def cin_tower(nc, ids, tables, w0a, w0b, f1, f2, dense_t, w_top1, b_top1, w_top2, b_top2, w_top3,
              consts, scratch, y):
    with ExitStack() as ctx:
        def sb(name, shape, dt=F32):
            return ctx.enter_context(nc.sbuf_tensor(name, shape, dt))

        def ps(name, shape):
            return ctx.enter_context(nc.psum_tensor(name, shape, F32))

        def sem(name):
            return ctx.enter_context(nc.semaphore(name))

        idx = sb("idx", [P, BT, F], I32)
        one = sb("one", [P, 1])
        idx_batch = sb("idx_batch", [P, F], I32)
        looked = sb("looked", [P, F, D])
        ext = sb("ext", [P, D, EXT])
        const_sb = sb("const_sb", [P, P + TB])
        identity = const_sb[:, 0:P]
        same_sample = const_sb[:, P:P + TB]
        ws_hi = sb("ws_hi", [KC, NC1 * M], F32R)
        ws_lo = sb("ws_lo", [KC, NC1 * M], F32R)
        w1_hi = sb("w1_hi", [P, F * M], F32R)
        w1_lo = sb("w1_lo", [P, F * M], F32R)
        w2 = sb("w2", [P, F, M])
        wt3 = sb("wt3", [P, H2 // P])
        bt1 = sb("bt1", [P, H1 // P])
        bt2 = sb("bt2", [P, H2 // P])
        e_pairs = sb("e_pairs", [P, GT, EXT])
        e_tile = sb("e_tile", [P, GT, EXT])
        pair_prod = sb("pair_prod", [P, 2, GT, KC])
        z_hi = sb("z_hi", [P, 2, GT * P], F32R)
        z_lo = sb("z_lo", [P, 2, GT * P], F32R)
        cur1 = sb("cur1", [P, GT * P])
        cur1_hi = sb("cur1_hi", [P, GT, P], F32R)
        cur1_lo = sb("cur1_lo", [P, GT, P], F32R)
        act_prod = sb("act_prod", [P, NA, BANK])
        act_sum = sb("act_sum", [P, BANK])
        pool_sum = sb("pool_sum", [P, 2, BANK])
        dve_acc = sb("dve_acc", [P, 2, FB, M])
        dve_fold = sb("dve_fold", [P, FB // 2, M])
        cur2 = sb("cur2", [P, 2, M])
        e_block = sb("e_block", [P, 2, FG, TB])
        gram = sb("gram", [P, FG, B])
        w1_raw = gram[:, 0:-(-F * M // B), :].rearrange("p a b -> p (a b)")[:, 0:F * M]
        ws_a = gram[0:KC, 34:36, :].rearrange("p a b -> p (a b)")[:, 0:NC1 * M]
        ws_b = gram[0:KC, 32:34, :].rearrange("p a b -> p (a b)")[:, 0:NC1 * M]
        z1 = sb("z1", [P, B])
        wt1 = sb("wt1", [P, 3, H1])
        wt2 = act_prod[:, H1 // P:H1 // P + 2, :].rearrange("p a (b n) -> p (a b) n", n=H2)
        dense = looked[0:NDENSE, :, :].rearrange("p f d -> p (f d)")[:, 0:B]
        wt1_dense = ext[0:NDENSE, :, :].rearrange("p d f -> p (d f)")[:, 0:H1]
        w2_hi, w2_lo = w1_hi, w1_lo
        gram_hi = [z_hi[:, 0, :], z_hi[:, 1, :], cur1_hi[:, :, :].rearrange("p q m -> p (q m)")]
        gram_lo = [z_lo[:, 0, :], z_lo[:, 1, :], cur1_lo[:, :, :].rearrange("p q m -> p (q m)")]
        h1 = act_prod[:, 0:H1 // P, :]
        h2 = dve_acc[:, :, :, :].rearrange("p c j m -> p c (j m)")
        z3 = act_sum
        y_sb = pool_sum[0:1, 0, :]

        l2 = [ps(f"l2_{r}", [P, BANK]) for r in range(RING)]
        xp = [ps(f"xp_{r}", [P, BANK]) for r in range(2)]
        l1 = ps("l1", [P, BANK])
        gm = ps("gm", [P, BANK])

        ids_in = sem("ids_in")
        consts_in = sem("consts_in")
        w0_in = sem("w0_in")
        w1_in = sem("w1_in")
        w2_in = sem("w2_in")
        weights_in = sem("weights_in")
        dense_in = sem("dense_in")
        top_in = sem("top_in")
        one_made = sem("one_made")
        idx_copied = sem("idx_copied")
        gathered = sem("gathered")
        ext_main = sem("ext_main")
        ext_made = sem("ext_made")
        first_written = sem("first_written")
        scratch_written = sem("scratch_written")
        e_pairs_in = sem("e_pairs_in")
        e_tile_in = [sem(f"e_tile_in_{q}") for q in range(GT)]
        ws_made = sem("ws_made")
        w1_hi_made = sem("w1_hi_made")
        w1_lo_made = sem("w1_lo_made")
        block_ones = sem("block_ones")
        pairs_made = sem("pairs_made")
        transposed = sem("transposed")
        z_copied = sem("z_copied")
        z_split = sem("z_split")
        layer1_chunks = sem("layer1_chunks")
        cur1_copied = sem("cur1_copied")
        z1_made = sem("z1_made")
        hi_made = sem("hi_made")
        lo_made = sem("lo_made")
        layer2_bank = sem("layer2_bank")
        act_products = sem("act_products")
        dve_products = sem("dve_products")
        pool_adds = sem("pool_adds")
        dve_adds = sem("dve_adds")
        dve_folds = sem("dve_folds")
        cur2_made = sem("cur2_made")
        block_made = sem("block_made")
        gram_done = sem("gram_done")
        gram_copied = sem("gram_copied")
        w2_hi_made = sem("w2_hi_made")
        w2_lo_made = sem("w2_lo_made")
        gram_hi_made = sem("gram_hi_made")
        gram_lo_made = sem("gram_lo_made")
        z3_fields = sem("z3_fields")
        z3_copied = sem("z3_copied")
        top1_done = sem("top1_done")
        h1_made = sem("h1_made")
        top2_done = sem("top2_done")
        h2_made = sem("h2_made")
        top3_done = sem("top3_done")
        y_copied = sem("y_copied")
        y_out = sem("y_out")

        block = ctx.enter_context(nc.Block())

        def wait(eng, s, value):
            if not (isinstance(value, int) and value <= 0):
                eng.wait_ge(s, value)

        def groups(eng, body):
            first, last = 1, NG - 3
            for i in range(first):
                body(i, lambda n: n < NT)
            with eng.Fori(first, last) as i:
                body(i, lambda n: True)
            for i in range(last, NG):
                body(i, lambda n: n < NT)

        def slots_before(group, c):
            return group * NC1 + (c - 1 if c >= 2 else -1 if c == 1 else 0)

        def chunk_shifts(c):
            return min(JC, SHIFTS - c * JC)

        def wait_then(eng, s, value):
            eng.wait_ge(ids_in, 16)
            wait(eng, s, value)

        def batches(eng, body):
            for m in range(BATCH):
                body(m, m, 0)
            with eng.Fori(1, BT - 1) as t:
                for s in range(BATCH):
                    body(t * BATCH + s, s, t)
            for m in range((BT - 1) * BATCH, NT + DEPTH):
                body(m, m % BATCH, BT - 1)

        def make_pairs(eng, product, group, c):
            if c == 0:
                eng.wait_ge(e_pairs_in, 16 * (group + 1))
            wait(eng, transposed, slots_before(group, c))
            kc = chunk_shifts(c)
            e = e_pairs[:, :, :]
            row = list(e.ap[0])
            product(pair_prod[:, c % 2, :, 0:kc * F].rearrange("p t (k f) -> p t k f", f=F),
                    bass.AP(e.tensor, e.offset, [row, [EXT, GT], [0, kc], [1, F]]),
                    bass.AP(e.tensor, e.offset + c * JC, [row, [EXT, GT], [1, kc], [1, F]]),
                    ALU.mult).then_inc(pairs_made, 1)

        scratch_rows = scratch.rearrange("b (d f) -> (b d) f", f=EXT)

        @block.sync
        def _(sp):
            sp.dma_start(idx[:, :, :], ids.rearrange("(t p) f -> p t f", p=P)).then_inc(ids_in, 16)
            sp.dma_start(w1_raw.rearrange("g (f h) -> g f h", h=M),
                         f1.rearrange("(f g) h -> g f h", g=M)).then_inc(w1_in, 16)
            sp.dma_start(w2[:, :, :], f2.rearrange("(f h) m -> h f m", h=M)).then_inc(w2_in, 16)

            def write_batch(t):
                wait_then(sp, ext_made, t + 1)
                sp.dma_start(scratch[bass.ds(t * P, P), :],
                             ext[:, :, :].rearrange("p d f -> p (d f)")).then_inc(scratch_written, 16)

            group_rows = scratch_rows.rearrange("(g t p) f -> g p t f", t=GT, p=P)

            def load_pairs(group):
                sp.dma_start(e_pairs[:, :, :], group_rows[bass.ds(group, 1), :, :, :]
                             .rearrange("a p t f -> (a p) t f")).then_inc(e_pairs_in, 16)

            def load_tile(n, q):
                sp.dma_start(e_tile[:, q, :], scratch_rows[bass.ds(n * P, P), :]).then_inc(e_tile_in[q], 16)

            def loads(m, s, batch):
                n = m - DEPTH
                if s == BATCH - 2 and (not isinstance(m, int) or m < NT - GT):
                    write_batch(batch + 1)
                if s % GT == GT - 1 and (not isinstance(m, int) or m < NT - GT):
                    if s == BATCH - 1:
                        sp.wait_ge(scratch_written, 16 * (batch + 2))
                    group = batch * (BATCH // GT) + s // GT + 1
                    wait_then(sp, pairs_made, group * NC1)
                    load_pairs(group)
                if not isinstance(m, int) or 0 <= n < NT - GT:
                    wait_then(sp, cur2_made, n + 1)
                    load_tile(n + GT, (s - DEPTH) % GT)

            sp.wait_ge(ext_made, 1)
            first = GT * TB
            sp.dma_start(scratch[0:first, :],
                         ext[0:first, :, :].rearrange("p d f -> p (d f)")).then_inc(first_written, 16)
            sp.dma_start(scratch[first:P, :],
                         ext[first:P, :, :].rearrange("p d f -> p (d f)")).then_inc(scratch_written, 16)
            sp.wait_ge(first_written, 16)
            load_pairs(0)
            for n in range(GT):
                load_tile(n, n)
            sp.wait_ge(scratch_written, 16)
            batches(sp, loads)
            sp.wait_ge(ext_made, BT)
            sp.wait_ge(scratch_written, 16 * BT)
            sp.dma_start(wt1_dense, w_top1[3 * M:, :]).then_inc(dense_in, 16)
            sp.dma_start(dense, dense_t).then_inc(dense_in, 16)
            sp.wait_ge(cur2_made, NT)
            sp.dma_start(wt2, w_top2.rearrange("(c p) n -> p c n", p=P)).then_inc(top_in, 16)
            sp.wait_ge(y_copied, 1)
            sp.dma_start(y.rearrange("b o -> o b"), y_sb).then_inc(y_out, 16)
            sp.wait_ge(y_out, 16)

        @block.gpsimd
        def _(pool):
            pool.wait_ge(ids_in, 16)

            def take_indices(t):
                wait_then(pool, ext_made, t)
                nc.gpsimd.tensor_copy(idx_batch[:, :], idx[:, bass.ds(t, 1), :]
                                      .rearrange("p a f -> p (a f)")).then_inc(idx_copied, 1)
                pool.wait_ge(idx_copied, t + 1)

            def gather(f):
                nc.gpsimd.indirect_dma_start(
                    out=looked[:, f, :], out_offset=None, in_=tables[f],
                    in_offset=bass.IndirectOffsetOnAxis(ap=idx_batch[:, f:f + 1], axis=0),
                ).then_inc(gathered, 16)

            def extend(t):
                pool.wait_ge(gathered, (t + 1) * 16 * F)
                wait(pool, scratch_written, t * 16)
                if isinstance(t, int) and t == 1:
                    pool.wait_ge(first_written, 16)
                for made, cols, n in ((ext_main, slice(0, F), F), (ext_made, slice(F, EXT), EXT - F)):
                    if made is ext_made:
                        pool.wait_ge(ext_main, t + 1)
                    nc.gpsimd.tensor_tensor(ext[:, :, cols], looked[:, 0:n, :].rearrange("p f d -> p d f"),
                                            one[:, :].unsqueeze(2).to_broadcast([P, D, n]),
                                            ALU.mult).then_inc(made, 1)

            def sum_act(n, par, a):
                adds = POOL_SUMS - 1
                pool.wait_ge(act_products, n * NA + a + 2)
                wait(pool, pool_adds, n * adds + a)
                if a == adds - 1:
                    wait(pool, dve_adds, (n - 1) * DVE_ADDS)
                nc.gpsimd.tensor_tensor(pool_sum[:, par, :] if a == adds - 1 else act_sum[:, :],
                                        act_sum[:, :] if a else act_prod[:, 0, :],
                                        act_prod[:, a + 1, :], ALU.add).then_inc(pool_adds, 1)

            take_indices(0)
            nc.gpsimd.memset(one[:, :], 1.0).then_inc(one_made, 1)
            for f in range(F):
                gather(f)
            pool.wait_ge(one_made, 1)

            def body(m, s, batch):
                n = m - DEPTH
                real = not isinstance(m, int)
                more = real or batch < BT - 1
                if more and s == 0:
                    take_indices(batch + 1)
                gathers = list(range(s * GATHERS, min(F, (s + 1) * GATHERS))) if more else []
                if more and s == BATCH - 2:
                    extend(batch + 1)
                if gathers and s > 0:
                    gather(gathers.pop(0))
                group = batch * (BATCH // GT) + s // GT
                pairs = real or L1_AHEAD * GT <= m < NT
                if pairs and PAIRS_EARLY[s % GT] is not None:
                    make_pairs(pool, nc.gpsimd.tensor_tensor, group, PAIRS_EARLY[s % GT])
                if real or n >= 0:
                    for a in range(POOL_SUMS - 1):
                        sum_act(n, (s - DEPTH) % 2, a)
                        if gathers:
                            gather(gathers.pop(0))
                for f in gathers:
                    gather(f)
                if pairs:
                    make_pairs(pool, nc.gpsimd.tensor_tensor, group, PAIRS_LATE[s % GT])

            batches(pool, body)
            for c, cols in enumerate(W2_CHUNKS):
                pool.wait_ge(w2_hi_made, c + 1)
                nc.gpsimd.tensor_tensor(w2_lo[:, cols], w2[:, :, :].rearrange("p f m -> p (f m)")[:, cols],
                                        w2_hi[:, cols].bitcast(F32), ALU.subtract).then_inc(w2_lo_made, 1)

        @block.scalar
        def _(act):
            act.dma_start(const_sb[:, :], consts).then_inc(consts_in, 16)
            act.dma_start(ws_a, w0a.rearrange("p c m -> p (c m)")).then_inc(w0_in, 16)
            act.dma_start(ws_b, w0b.rearrange("p c m -> p (c m)")).then_inc(w0_in, 16)
            act.dma_start(wt1[:, :, :], w_top1[0:3 * M, :]
                          .rearrange("(c p) n -> p c n", p=P)).then_inc(weights_in, 16)
            act.dma_start(wt3[:, :], w_top3).then_inc(weights_in, 16)
            act.dma_start(bt1[:, :], b_top1).then_inc(weights_in, 16)
            act.dma_start(bt2[:, :], b_top2).then_inc(weights_in, 16)
            act.wait_ge(w1_in, 16)
            nc.scalar.copy(w1_hi[:, :], w1_raw).then_inc(w1_hi_made, 1)

            def copy_z(group, c):
                wait(act, layer1_chunks, slots_before(group, c))
                act.wait_ge(transposed, group * NC1 + c + 1)
                k = chunk_shifts(c) * F
                nc.scalar.copy(z_hi[0:k, c % 2, :], xp[c % 2][0:k, :]).then_inc(z_copied, 1)

            def copy_cur1(group):
                act.wait_ge(layer1_chunks, (group + 1) * NC1)
                wait(act, lo_made, GT * group)
                wait(act, z1_made, group)
                nc.scalar.copy(cur1[:, :], l1[:, :]).then_inc(cur1_copied, 1)

            def copy_gram(n):
                act.wait_ge(gram_done, n + 1)
                if isinstance(n, int) and n == 0:
                    act.wait_ge(w1_lo_made, 1)
                nc.scalar.copy(gram[:, :, bass.ds(n * TB, TB)],
                               gm[:, 0:FG * TB].rearrange("p (f b) -> p f b", b=TB)).then_inc(gram_copied, 1)

            def body(i, there):
                for q in range(GT):
                    n = i * GT + q
                    act.wait_ge(e_tile_in[q], 16 * (i + 1))
                    first = isinstance(n, int) and n == 0
                    second_group = list(range(NC1)) if first else []
                    for r, b in enumerate(ACT_BANKS):
                        while second_group and second_group[0] < b:
                            copy_z(1, second_group.pop(0))
                        act.wait_ge(layer2_bank, n * NB + b + 1)
                        if r < POOL_SUMS:
                            wait(act, pool_adds, (n - 1) * (POOL_SUMS - 1) + max(r, 1))
                        else:
                            wait(act, dve_adds, (n - 1) * DVE_ADDS + r - POOL_SUMS + 1)
                        for j, f in enumerate(fields(b)):
                            last = nc.scalar.activation(act_prod[:, r, j * M:(j + 1) * M],
                                                        l2[(q * NB + b) % RING][:, j * M:(j + 1) * M],
                                                        ACT.Copy, scale=e_tile[:, q, f:f + 1])
                        last.then_inc(act_products, 1)
                        if b == GRAM_COPY and not (isinstance(n, int) and n < GRAM_LAG):
                            copy_gram(n - GRAM_LAG)
                        if r == (NA - 1 if first else COPY_CUR1) and q == 0 and there(n + GT):
                            copy_cur1(i + 1)
                        for at, c in chunks_beside(i)[0].items():
                            if (at[0] == q and (r == 0 or at[1] > ACT_BANKS[r - 1])
                                    and at[1] <= b and there(n + L1_AHEAD * GT)):
                                copy_z(i + L1_AHEAD, c)

            for c in range(NC1):
                copy_z(0, c)
            copy_cur1(0)
            groups(act, body)
            act.wait_ge(w2_in, 16)
            act.wait_ge(layer2_bank, NT * NB)
            for c, cols in enumerate(W2_CHUNKS):
                nc.scalar.copy(w2_hi[:, cols],
                               w2[:, :, :].rearrange("p f m -> p (f m)")[:, cols]).then_inc(w2_hi_made, 1)
                if c < 2:
                    copy_gram(NT - 2 + c)
            act.wait_ge(gram_copied, NT)
            for f in range(F):
                wait(act, z3_fields, f - len(gram_hi) + 1)
                nc.scalar.copy(gram_hi[f % len(gram_hi)], gram[:, f, :]).then_inc(gram_hi_made, 1)
            act.wait_ge(z3_fields, F)
            nc.scalar.copy(z3[:, :], gm[:, :]).then_inc(z3_copied, 1)
            act.wait_ge(weights_in, 16 * 4)
            for c in range(H1 // P):
                act.wait_ge(top1_done, c + 1)
                nc.scalar.activation(h1[:, c, :], l2[c][:, :], ACT.Relu, bias=bt1[:, c:c + 1]).then_inc(h1_made, 1)
            for c in range(H2 // P):
                act.wait_ge(top2_done, c + 1)
                nc.scalar.activation(h2[:, c, :], xp[c][:, :], ACT.Relu, bias=bt2[:, c:c + 1]).then_inc(h2_made, 1)
            act.wait_ge(top3_done, 1)
            nc.scalar.copy(y_sb, l1[0:1, :]).then_inc(y_copied, 1)

        @block.vector
        def _(dve):
            dve.wait_ge(w0_in, 32)
            nc.vector.tensor_tensor(ws_a, ws_a, ws_b, ALU.add).then_inc(ws_made, 1)
            dve.wait_ge(ws_made, 1)
            nc.vector.tensor_copy(ws_hi[:, :], ws_a).then_inc(ws_made, 1)
            dve.wait_ge(ws_made, 2)
            nc.vector.tensor_tensor(ws_lo[:, :], ws_a, ws_hi[:, :].bitcast(F32), ALU.subtract).then_inc(ws_made, 1)
            dve.wait_ge(consts_in, 16)
            for par in range(2):
                nc.vector.tensor_copy(e_block[:, par, F, :], same_sample).then_inc(block_ones, 1)
            dve.wait_ge(w1_hi_made, 1)
            nc.vector.tensor_tensor(w1_lo[:, :], w1_raw, w1_hi[:, :].bitcast(F32),
                                    ALU.subtract).then_inc(w1_lo_made, 1)

            def split_hi(n, q, group):
                dve.wait_ge(cur1_copied, group + 1)
                wait(dve, layer2_bank, (n - GT + 1) * NB)
                nc.vector.tensor_copy(cur1_hi[:, q, :], cur1[:, q * P:(q + 1) * P]).then_inc(hi_made, 1)

            def split_lo(n, q):
                dve.wait_ge(hi_made, n + 1)
                nc.vector.tensor_tensor(cur1_lo[:, q, :], cur1[:, q * P:(q + 1) * P],
                                        cur1_hi[:, q, :].bitcast(F32), ALU.subtract).then_inc(lo_made, 1)

            def split_z(group, c):
                wait(dve, layer1_chunks, slots_before(group, c))
                dve.wait_ge(z_copied, group * NC1 + c + 1)
                k = chunk_shifts(c) * F
                nc.vector.tensor_tensor(z_lo[0:k, c % 2, :], xp[c % 2][0:k, :],
                                        z_hi[0:k, c % 2, :].bitcast(F32), ALU.subtract).then_inc(z_split, 1)

            def sum_cur1(group):
                nc.vector.tensor_reduce(z1[:, bass.ts(group, GT * TB)],
                                        cur1[:, :].rearrange("p (b d) -> p b d", d=D),
                                        AX.X, ALU.add).then_inc(z1_made, 1)

            dve.wait_ge(gathered, 16 * F)
            nc.vector.tensor_copy(ext[:, :, 0:F], looked[:, :, :].rearrange("p f d -> p d f")).then_inc(ext_main, 1)
            dve.wait_ge(ext_main, 1)
            nc.vector.tensor_copy(ext[:, :, F:EXT], looked[:, 0:EXT - F, :]
                                  .rearrange("p f d -> p d f")).then_inc(ext_made, 1)
            for c in range(2):
                make_pairs(dve, nc.vector.tensor_tensor, 0, c)
            for c in range(NC1):
                if c + 2 < NC1:
                    make_pairs(dve, nc.vector.tensor_tensor, 0, c + 2)
                split_z(0, c)
            for c in range(2):
                make_pairs(dve, nc.vector.tensor_tensor, 1, c)
            for n in range(GT - 1):
                split_hi(n, n, 0)
                split_lo(n, n)
            sum_cur1(0)

            def add_banks(n, par, r, share):
                if r == 0:
                    dve.wait_ge(dve_products, (n + 1) * DVE_PER_TILE)
                else:
                    dve.wait_ge(dve_adds, n * DVE_ADDS + r)
                acc = dve_acc[:, par, :, :].rearrange("p j m -> p (j m)")
                nc.vector.tensor_tensor(acc, acc, share, ALU.add).then_inc(dve_adds, 1)

            def close(n, par, step):
                if step < NA - POOL_SUMS:
                    dve.wait_ge(act_products, n * NA + POOL_SUMS + step + 1)
                    add_banks(n, par, step, act_prod[:, POOL_SUMS + step, :])
                elif step == DVE_ADDS - 1:
                    dve.wait_ge(pool_adds, (n + 1) * (POOL_SUMS - 1))
                    add_banks(n, par, step, pool_sum[:, par, :])
                elif step == DVE_ADDS:
                    dve.wait_ge(dve_adds, (n + 1) * DVE_ADDS)
                    nc.vector.tensor_tensor(dve_fold[:, :, :], dve_acc[:, par, 0:FB // 2, :],
                                            dve_acc[:, par, FB // 2:FB, :], ALU.add).then_inc(dve_folds, 1)
                elif step == DVE_ADDS + 1:
                    dve.wait_ge(dve_folds, n + 1)
                    wait(dve, gram_done, n - 1)
                    nc.vector.tensor_tensor(cur2[:, par, :], dve_fold[:, 0, :], dve_fold[:, 1, :],
                                            ALU.add).then_inc(cur2_made, 1)

            def make_block(n, par, q):
                wait(dve, gram_done, n - 1)
                nc.vector.tensor_tensor(e_block[:, par, 0:F, :],
                                        e_tile[:, q, 0:F].unsqueeze(2).to_broadcast([P, F, TB]),
                                        same_sample.unsqueeze(1).to_broadcast([P, F, TB]),
                                        ALU.mult).then_inc(block_made, 1)

            def body(i, there):
                for q in range(GT):
                    n = i * GT + q
                    par = q % 2
                    dve.wait_ge(e_tile_in[q], 16 * (i + 1))
                    done = 0
                    second_group = list(range(NC1)) if isinstance(n, int) and n == 0 else []
                    for r, b in enumerate(DVE_BANKS):
                        while second_group and second_group[0] < b:
                            c = second_group.pop(0)
                            if c + 2 < NC1:
                                make_pairs(dve, nc.vector.tensor_tensor, 1, c + 2)
                            split_z(1, c)
                        dve.wait_ge(layer2_bank, n * NB + b + 1)
                        for j, f in enumerate(fields(b)):
                            acc = dve_acc[:, par, j, :]
                            part = l2[(q * NB + b) % RING][:, j * M:(j + 1) * M]
                            if r == 0:
                                nc.vector.tensor_scalar(acc, part, e_tile[:, q, f:f + 1], None,
                                                        ALU.mult).then_inc(dve_products, 1)
                            else:
                                dve.wait_ge(dve_products, n * DVE_PER_TILE + done - FB + 1)
                                nc.vector.scalar_tensor_tensor(acc, part, e_tile[:, q, f:f + 1], acc,
                                                               ALU.mult, ALU.add).then_inc(dve_products, 1)
                            done += 1
                        for at, c in chunks_beside(i)[0].items():
                            if split_after(*at) == (q, b) and there((i + L1_AHEAD) * GT):
                                split_z(i + L1_AHEAD, c)
                        if not (isinstance(n, int) and n == 0):
                            for step in CLOSE_AFTER[r]:
                                close(n - 1, 1 - par, step)
                        if r == 1 and there(n + GT - 1):
                            split_hi(n + GT - 1, (q + GT - 1) % GT, i + (q + GT - 1) // GT)
                        if r == 2 and there(n + GT - 1):
                            split_lo(n + GT - 1, (q + GT - 1) % GT)
                        if r == BLOCK_RANK:
                            make_block(n, par, q)
                        if r == 3 and q == 1 and there(n + GT):
                            sum_cur1(i + 1)

            groups(dve, body)
            for step in range(DVE_ADDS + 2):
                close(NT - 1, 1, step)
            for f in range(F):
                dve.wait_ge(gram_hi_made, f + 1)
                nc.vector.tensor_tensor(gram_lo[f % len(gram_lo)], gram[:, f, :],
                                        gram_hi[f % len(gram_hi)].bitcast(F32),
                                        ALU.subtract).then_inc(gram_lo_made, 1)

        @block.tensor
        def _(pe):
            def transpose(group, c):
                pe.wait_ge(pairs_made, group * NC1 + c + 1)
                wait(pe, z_split, slots_before(group, c))
                k = chunk_shifts(c) * F
                for t in range(GT):
                    last = nc.tensor.transpose(xp[c % 2][0:k, t * P:(t + 1) * P],
                                               pair_prod[:, c % 2, t, 0:k], identity)
                last.then_inc(transposed, 1)

            def layer1(group, c):
                if c == 0:
                    wait(pe, cur1_copied, group)
                pe.wait_ge(z_split, group * NC1 + c + 1)
                k = chunk_shifts(c) * F
                cols = slice(c * M, (c + 1) * M)
                nc.tensor.matmul(l1[:, :], ws_lo[0:k, cols], z_hi[0:k, c % 2, :], start=(c == 0), stop=False)
                nc.tensor.matmul(l1[:, :], ws_hi[0:k, cols], z_lo[0:k, c % 2, :], start=False, stop=False)
                nc.tensor.matmul(l1[:, :], ws_hi[0:k, cols], z_hi[0:k, c % 2, :], start=False,
                                 stop=(c == NC1 - 1)).then_inc(layer1_chunks, 1)

            def chunk_step(group, c):
                if c < NC1:
                    transpose(group, c)
                if c > 0:
                    layer1(group, c - 1)

            def gram_tile(n, par):
                pe.wait_ge(cur2_made, n + 1)
                pe.wait_ge(block_made, n + 1)
                if isinstance(n, int) and n < 2:
                    pe.wait_ge(block_ones, 2)
                wait(pe, gram_copied, n)
                nc.tensor.matmul(gm[:, 0:FG * TB], cur2[:, par, :],
                                 e_block[:, par, :, :].rearrange("p f b -> p (f b)"),
                                 start=True, stop=True).then_inc(gram_done, 1)

            def bank_is_free(n, b):
                dn, b = (0, b - RING) if b >= RING else (-1, b - RING + NB)
                if b in ACT_BANKS:
                    wait(pe, act_products, (n + dn) * NA + ACT_BANKS.index(b) + 1)
                else:
                    wait(pe, dve_products, (n + dn) * DVE_PER_TILE + dve_products_through(b))

            pe.wait_ge(consts_in, 16)
            pe.wait_ge(ws_made, 3)
            for c in range(NC1 + 1):
                chunk_step(0, c)
            pe.wait_ge(w1_lo_made, 1)

            def body(i, there):
                for q in range(GT):
                    n = i * GT + q
                    pe.wait_ge(lo_made, n + 1)
                    for b in range(NB):
                        bank = l2[(q * NB + b) % RING]
                        bank_is_free(n, b)
                        cols = slice(b * BANK, b * BANK + len(fields(b)) * M)
                        out = bank[:, 0:len(fields(b)) * M]
                        nc.tensor.matmul(out, cur1_hi[:, q, :], w1_lo[:, cols], start=True, stop=False)
                        nc.tensor.matmul(out, cur1_lo[:, q, :], w1_hi[:, cols], start=False, stop=False)
                        nc.tensor.matmul(out, cur1_hi[:, q, :], w1_hi[:, cols], start=False,
                                         stop=True).then_inc(layer2_bank, 1)
                        if b == GRAM_AFTER and not (isinstance(n, int) and n < GRAM_LAG):
                            gram_tile(n - GRAM_LAG, (q + GRAM_LAG) % 2)
                        if isinstance(n, int) and n == 0 and b <= NC1:
                            chunk_step(1, b)
                        transpose_at, layer1_at = chunks_beside(i)
                        if there(n + L1_AHEAD * GT):
                            if (q, b) in transpose_at:
                                transpose(i + L1_AHEAD, transpose_at[q, b])
                            if (q, b) in layer1_at:
                                layer1(i + L1_AHEAD, layer1_at[q, b])

            groups(pe, body)

            def top1(weights, x, start=False, stop=False, chunks=range(H1 // P)):
                for c in chunks:
                    if start:
                        bank_is_free(NT, c)
                    last = nc.tensor.matmul(l2[c][:, :], weights[:, c * P:(c + 1) * P], x, start=start, stop=stop)
                    if stop:
                        last.then_inc(top1_done, 1)

            pe.wait_ge(weights_in, 16 * 4)
            pe.wait_ge(z1_made, NG)
            top1(wt1[:, 0, :], z1[:, :], start=True)
            gram_tile(NT - 2, 0)
            pe.wait_ge(dense_in, 16 * 2)
            top1(wt1_dense, dense, chunks=range(2))
            gram_tile(NT - 1, 1)
            top1(wt1_dense, dense, chunks=range(2, H1 // P))
            pe.wait_ge(gram_copied, NT)
            top1(wt1[:, 1, :], gram[:, F, :])

            for f in range(F):
                cols = slice(f * M, (f + 1) * M)
                hi, lo = gram_hi[f % len(gram_hi)], gram_lo[f % len(gram_lo)]
                pe.wait_ge(w2_lo_made, f // SPLIT_FIELDS + 1)
                pe.wait_ge(gram_hi_made, f + 1)
                nc.tensor.matmul(gm[:, :], w2_lo[:, cols], hi, start=(f == 0), stop=False)
                nc.tensor.matmul(gm[:, :], w2_hi[:, cols], hi, start=False, stop=False)
                pe.wait_ge(gram_lo_made, f + 1)
                nc.tensor.matmul(gm[:, :], w2_hi[:, cols], lo, start=False, stop=(f == F - 1)).then_inc(z3_fields, 1)
            pe.wait_ge(z3_copied, 1)
            top1(wt1[:, 2, :], z3[:, :], stop=True)
            pe.wait_ge(top_in, 16)
            for c in range(H2 // P):
                for k in range(H1 // P):
                    pe.wait_ge(h1_made, k + 1)
                    last = nc.tensor.matmul(xp[c][:, :], wt2[:, k, c * P:(c + 1) * P], h1[:, k, :],
                                            start=(k == 0), stop=(k == H1 // P - 1))
                last.then_inc(top2_done, 1)
            for c in range(H2 // P):
                pe.wait_ge(h2_made, c + 1)
                last = nc.tensor.matmul(l1[0:1, :], wt3[:, c:c + 1], h2[:, c, :], start=(c == 0),
                                        stop=(c == H2 // P - 1))
            last.then_inc(top3_done, 1)


def kernel(**inputs):
    import numpy as np
    import concourse.bacc as bacc
    from concourse.bass_utils import run_bass_kernel_spmd

    nc = bacc.Bacc("TRN2", target_bir_lowering=False, num_devices=1)
    arrays = {}

    def given(name, a):
        a = np.ascontiguousarray(a)
        arrays[name] = a
        return nc.dram_tensor(name, a.shape, mybir.dt.from_np(a.dtype), kind="ExternalInput").ap()

    f0 = np.asarray(inputs["L0_rec_f0"])
    c, j, f = np.meshgrid(np.arange(NC1), np.arange(JC), np.arange(F), indexing="ij")
    k = JC * c + j
    other = (f + k) % F
    padded = np.concatenate([f0, np.zeros((1, M), f0.dtype)])
    one = np.where(k < SHIFTS, f * F + other, F * F).reshape(NC1, KC).T
    two = np.where((k < SHIFTS) & (k > 0), other * F + f, F * F).reshape(NC1, KC).T
    consts = np.concatenate([np.eye(P, dtype=np.float32),
                             np.repeat(np.eye(TB, dtype=np.float32), D, axis=0)], axis=1)
    args = dict(
        ids=given("ids", inputs["ids"]),
        tables=[given(f"tbl_{t}", inputs[f"tbl_{t}"]) for t in range(F)],
        w0a=given("w0a", padded[one]),
        w0b=given("w0b", padded[two]),
        f1=given("f1", inputs["L0_rec_f1"]),
        f2=given("f2", inputs["L0_rec_f2"]),
        dense_t=given("dense_t", np.asarray(inputs["dense_ctx"]).T),
        w_top1=given("w_top1", inputs["W_top1"]),
        b_top1=given("b_top1", np.asarray(inputs["b_top1"]).reshape(H1 // P, P).T),
        w_top2=given("w_top2", inputs["W_top2"]),
        b_top2=given("b_top2", np.asarray(inputs["b_top2"]).reshape(H2 // P, P).T),
        w_top3=given("w_top3", np.asarray(inputs["W_top3"]).reshape(H2 // P, P).T),
        consts=given("consts", consts),
        scratch=nc.dram_tensor("scratch", (B, D * EXT), F32, kind="Internal").ap(),
        y=nc.dram_tensor("y", (B, 1), F32, kind="ExternalOutput").ap(),
    )
    cin_tower(nc, **args)
    r = run_bass_kernel_spmd(nc, [arrays], core_ids=[0])
    return r.results[0]["y"]
```
